# Optimizing a Trainium2 kernel written in Bass

```python
import numpy as np
import jax
import jax.numpy as jnp

def _softmax(x, axis=-1):
    return jax.nn.softmax(x, axis=axis)

def _gelu(x):
    return jax.nn.gelu(x, approximate=True)

def _silu(x):
    return jax.nn.silu(x)

def _sigmoid(x):
    return jax.nn.sigmoid(x)

def _layernorm(x, axis=-1, eps=1e-05):
    m = jnp.mean(x, axis=axis, keepdims=True)
    v = jnp.var(x, axis=axis, keepdims=True)
    return (x - m) / jnp.sqrt(v + eps)

def _scatter_add(tgt, idx, src, axis=0):
    return tgt.at[idx].add(src)

def _segment_sum(src, seg, n):
    return jax.ops.segment_sum(src, seg, n)
kernel_name = 'mk_flamingo_gated_d2_seqx_r8_cc2f31'

def setup_inputs(seed: int=0):
    np.random.seed(seed)
    _w = jnp.asarray

    def _rec_inputs():
        import jax
        import jax.numpy as jnp
        _rk = jax.random.key(seed)
        x = 0.5 + 0.2887 * jax.random.normal(jax.random.fold_in(_rk, 1), (4, 256, 256), jnp.float32)
        _lenS = 256 - jax.random.randint(jax.random.fold_in(_rk, 7), (4,), 0, max(1, 256 // 4) + 1, jnp.int32)
        _lenS2 = 256 - jax.random.randint(jax.random.fold_in(_rk, 8), (4,), 0, max(1, 256 // 4) + 1, jnp.int32)
        _ctx_512P = jax.random.normal(jax.random.fold_in(_rk, 11), (4, 16, 64), jnp.float32)
        _ctx_512c = jax.random.dirichlet(jax.random.fold_in(_rk, 511), 0.3 * jnp.ones((16,), jnp.float32), (4, 256))
        _ctx_512t = jnp.einsum('bsk,bkd->bsd', _ctx_512c, _ctx_512P)
        _ctx_512t = _ctx_512t * jax.lax.rsqrt(jnp.mean(jnp.square(_ctx_512t)) + 1e-12) * 0.953939
        ctx_512 = -0.000392918 + 0.999932 * (_ctx_512t + 0.3 * jax.random.normal(jax.random.fold_in(_rk, 611), (4, 256, 64), jnp.float32))
        _g = jax.random.normal(jax.random.fold_in(_rk, 9001), (2, 2), jnp.float32)
        _g = jnp.sign(_g) * jnp.maximum(jnp.abs(_g), 1.0) + (_g == 0) * 1.0
        g_xattn = _g[0]
        g_ffn = _g[1]
        return (x, ctx_512, g_xattn, g_ffn)
    x, ctx_512, g_xattn, g_ffn = _rec_inputs()

    def _L0_xattn_setup():
        import jax, jax.numpy as jnp
        import numpy as np
        B, N, D = (16, 256, 64)
        H = 4
        TOP_K_RATIO = 0.3
        key = jax.random.key(seed)
        k1, k2, k3, k4 = jax.random.split(key, 4)
        h = jax.random.normal(k1, (B, N, D), dtype=jnp.float32)
        adj_raw = jax.random.uniform(k2, (B, N, N), dtype=jnp.float32)
        lim = 1.0 / np.sqrt(D)
        Wq = jax.random.uniform(k3, (D, D), minval=-lim, maxval=lim, dtype=jnp.float32)
        Wk = jax.random.uniform(k4, (D, D), minval=-lim, maxval=lim, dtype=jnp.float32)
        gamma_raw = jnp.float32(-0.85)
        return {'h': h, 'adj_raw': adj_raw, 'Wq': Wq, 'Wk': Wk, 'gamma_raw': gamma_raw}
    _L0_xattn_all = _L0_xattn_setup()
    _L0_xattn_in = {k: v for k, v in _L0_xattn_all.items() if k in ('Wq', 'Wk', 'gamma_raw')}
    del _L0_xattn_all

    def _L0_ffn_setup():
        import jax, jax.numpy as jnp
        import numpy as np
        TOP_K = 2
        key = jax.random.key(seed)
        ks = jax.random.split(key, 6)
        B, S, H, F, E = (1, 256, 256, 176, 8)
        Fs = 2 * F
        std = jnp.float32(0.02)
        return {'hidden_states': jax.random.normal(ks[0], (B, S, H), jnp.float32), 'gate_weight': jax.random.normal(ks[1], (E, H), jnp.float32) * std, 'gate_up_weights': jax.random.normal(ks[2], (E, 2 * F, H), jnp.float32) * std, 'down_weights': jax.random.normal(ks[3], (E, H, F), jnp.float32) * std, 'shared_gate_up': jax.random.normal(ks[4], (2 * Fs, H), jnp.float32) * std, 'shared_down': jax.random.normal(ks[5], (H, Fs), jnp.float32) * std}
    _L0_ffn_all = _L0_ffn_setup()
    _L0_ffn_in = {k: v for k, v in _L0_ffn_all.items() if k in ('gate_weight', 'gate_up_weights', 'down_weights', 'shared_gate_up', 'shared_down')}
    del _L0_ffn_all

    def _L1_xattn_setup():
        import jax, jax.numpy as jnp
        import numpy as np
        B, S, L = (2, 128, 128)
        DIM_Q, H, K, D_C, D_CQ, R = (256, 16, 128, 64, 192, 64)

        def _rope_tables(length, dim):
            inv = 1.0 / 10000.0 ** (jnp.arange(0, dim, 2, dtype=jnp.float32) / dim)
            f = jnp.arange(length, dtype=jnp.float32)[:, None] * inv[None, :]
            sin = jnp.repeat(jnp.sin(f), 2, axis=-1)
            cos = jnp.repeat(jnp.cos(f), 2, axis=-1)
            return (sin, cos)

        def _rotate_half(x):
            half = x.shape[-1] // 2
            return jnp.concatenate([-x[..., half:], x[..., :half]], axis=-1)

        def _apply_rope(x, sin, cos):
            return x * cos + _rotate_half(x) * sin
        key = jax.random.key(seed)
        ks = jax.random.split(key, 8)
        return {'hidden_q': jax.random.normal(ks[0], (B, S, DIM_Q), jnp.float32), 'kv_c': jax.random.normal(ks[1], (B, L, D_C), jnp.float32), 'Wq': jax.random.normal(ks[2], (H * K, DIM_Q), jnp.float32) / np.sqrt(DIM_Q).astype(np.float32), 'w_kc_q': jax.random.normal(ks[3], (H, K, D_CQ), jnp.float32) / np.sqrt(K).astype(np.float32), 'w_kc_kv': jax.random.normal(ks[4], (H, K, D_C), jnp.float32) / np.sqrt(K).astype(np.float32), 'W_qr': jax.random.normal(ks[5], (H, D_CQ, R), jnp.float32) / np.float32(np.sqrt(D_CQ) * np.sqrt(R)), 'W_kr': jax.random.normal(ks[6], (H, D_C, R), jnp.float32) / np.sqrt(D_C).astype(np.float32), 'Wo': jax.random.normal(ks[7], (DIM_Q, H * K), jnp.float32) / np.sqrt(H * K).astype(np.float32)}
    _L1_xattn_all = _L1_xattn_setup()
    _L1_xattn_in = {k: v for k, v in _L1_xattn_all.items() if k in ('Wq', 'w_kc_q', 'w_kc_kv', 'W_qr', 'W_kr', 'Wo')}
    del _L1_xattn_all

    def _L1_ffn_setup():
        import jax, jax.numpy as jnp
        import numpy as np
        B, S, H = (1, 128, 256)
        F = 128
        E = 16
        K = 2
        NS = 1
        ROUTE_SCALE = 1.0
        key = jax.random.key(seed)
        ks = jax.random.split(key, 8)

        def w(k, shape, fan_in):
            return jax.random.normal(k, shape, jnp.float32) * fan_in ** (-0.5)
        return {'hidden_states': jax.random.normal(ks[0], (B, S, H), jnp.float32), 'gate_w': w(ks[1], (H, E), H), 'expert_bias': jnp.zeros((E,), jnp.float32), 'shared_gate_w': w(ks[2], (H, F * NS), H), 'shared_up_w': w(ks[3], (H, F * NS), H), 'shared_down_w': w(ks[4], (F * NS, H), F * NS), 'experts_gate_up': w(ks[5], (E, H, 2 * F), H), 'experts_down': w(ks[6], (E, F, H), F)}
    _L1_ffn_all = _L1_ffn_setup()
    _L1_ffn_in = {k: v for k, v in _L1_ffn_all.items() if k in ('gate_w', 'expert_bias', 'shared_gate_w', 'shared_up_w', 'shared_down_w', 'experts_gate_up', 'experts_down')}
    del _L1_ffn_all
    return {'x': x, 'ctx_512': ctx_512, 'g_xattn': g_xattn, 'g_ffn': g_ffn, 'L0_xattn_Wq': _L0_xattn_in['Wq'], 'L0_xattn_Wk': _L0_xattn_in['Wk'], 'L0_xattn_gamma_raw': _L0_xattn_in['gamma_raw'], 'L0_ffn_gate_weight': _L0_ffn_in['gate_weight'], 'L0_ffn_gate_up_weights': _L0_ffn_in['gate_up_weights'], 'L0_ffn_down_weights': _L0_ffn_in['down_weights'], 'L0_ffn_shared_gate_up': _L0_ffn_in['shared_gate_up'], 'L0_ffn_shared_down': _L0_ffn_in['shared_down'], 'L1_xattn_Wq': _L1_xattn_in['Wq'], 'L1_xattn_w_kc_q': _L1_xattn_in['w_kc_q'], 'L1_xattn_w_kc_kv': _L1_xattn_in['w_kc_kv'], 'L1_xattn_W_qr': _L1_xattn_in['W_qr'], 'L1_xattn_W_kr': _L1_xattn_in['W_kr'], 'L1_xattn_Wo': _L1_xattn_in['Wo'], 'L1_ffn_gate_w': _L1_ffn_in['gate_w'], 'L1_ffn_expert_bias': _L1_ffn_in['expert_bias'], 'L1_ffn_shared_gate_w': _L1_ffn_in['shared_gate_w'], 'L1_ffn_shared_up_w': _L1_ffn_in['shared_up_w'], 'L1_ffn_shared_down_w': _L1_ffn_in['shared_down_w'], 'L1_ffn_experts_gate_up': _L1_ffn_in['experts_gate_up'], 'L1_ffn_experts_down': _L1_ffn_in['experts_down']}

def reference(x, ctx_512, g_xattn, g_ffn, L0_xattn_Wq, L0_xattn_Wk, L0_xattn_gamma_raw, L0_ffn_gate_weight, L0_ffn_gate_up_weights, L0_ffn_down_weights, L0_ffn_shared_gate_up, L0_ffn_shared_down, L1_xattn_Wq, L1_xattn_w_kc_q, L1_xattn_w_kc_kv, L1_xattn_W_qr, L1_xattn_W_kr, L1_xattn_Wo, L1_ffn_gate_w, L1_ffn_expert_bias, L1_ffn_shared_gate_w, L1_ffn_shared_up_w, L1_ffn_shared_down_w, L1_ffn_experts_gate_up, L1_ffn_experts_down):
    import jax
    import jax.numpy as jnp

    def _L0_xattn_ref(h, adj_raw, Wq, Wk, gamma_raw):
        import jax, jax.numpy as jnp
        import numpy as np
        B, N, D = (16, 256, 64)
        H = 4
        TOP_K_RATIO = 0.3
        b, n, dm = h.shape
        d = dm // H
        Q = (h @ Wq.T).reshape(b, n, H, d).transpose(0, 2, 1, 3)
        K = (h @ Wk.T).reshape(b, n, H, d).transpose(0, 2, 1, 3)
        sim = jnp.einsum('bhnd,bhmd->bnm', Q, K) / (jnp.sqrt(jnp.float32(d)) * H)
        k = max(1, int(n * TOP_K_RATIO))
        topk_vals = jax.lax.top_k(sim, k)[0]
        threshold = topk_vals[:, :, -1:]
        sparse_mask = (sim >= threshold).astype(sim.dtype)
        A_learned = jax.nn.sigmoid(sim) * sparse_mask
        A_learned = (A_learned + jnp.swapaxes(A_learned, -1, -2)) * 0.5
        gamma = jax.nn.sigmoid(gamma_raw)
        return (1.0 - gamma) * adj_raw + gamma * A_learned

    def _L0_ffn_ref(hidden_states, gate_weight, gate_up_weights, down_weights, shared_gate_up, shared_down):
        import jax, jax.numpy as jnp
        import numpy as np
        TOP_K = 2
        B, S, H = hidden_states.shape
        E, twoF, _ = gate_up_weights.shape
        F = twoF // 2
        T = B * S
        x = hidden_states.reshape(T, H)
        logits = x @ gate_weight.T
        scores = jax.nn.softmax(logits, axis=-1)
        topk_w, topk_idx = jax.lax.top_k(scores, TOP_K)
        combine = jnp.zeros((T, E), x.dtype).at[jnp.arange(T)[:, None], topk_idx].add(topk_w)
        gu = jnp.einsum('th,efh->tef', x, gate_up_weights)
        act = jax.nn.silu(gu[..., :F]) * gu[..., F:]
        y = jnp.einsum('tef,te,ehf->th', act, combine, down_weights)
        Fs = shared_gate_up.shape[0] // 2
        sgu = x @ shared_gate_up.T
        sact = jax.nn.silu(sgu[:, :Fs]) * sgu[:, Fs:]
        y = y + sact @ shared_down.T
        return y.reshape(B, S, H)

    def _L1_xattn_ref(hidden_q, kv_c, Wq, w_kc_q, w_kc_kv, W_qr, W_kr, Wo):
        import jax, jax.numpy as jnp
        import numpy as np
        B, S, L = (2, 128, 128)
        DIM_Q, H, K, D_C, D_CQ, R = (256, 16, 128, 64, 192, 64)

        def _rope_tables(length, dim):
            inv = 1.0 / 10000.0 ** (jnp.arange(0, dim, 2, dtype=jnp.float32) / dim)
            f = jnp.arange(length, dtype=jnp.float32)[:, None] * inv[None, :]
            sin = jnp.repeat(jnp.sin(f), 2, axis=-1)
            cos = jnp.repeat(jnp.cos(f), 2, axis=-1)
            return (sin, cos)

        def _rotate_half(x):
            half = x.shape[-1] // 2
            return jnp.concatenate([-x[..., half:], x[..., :half]], axis=-1)

        def _apply_rope(x, sin, cos):
            return x * cos + _rotate_half(x) * sin
        Bv, Sv, _ = hidden_q.shape
        _, Lv, _ = kv_c.shape
        q_hk = (hidden_q @ Wq.T).reshape(Bv, Sv, H, K)
        q_big = jnp.einsum('bshk,hkq->bshq', q_hk, w_kc_q)
        sin_q, cos_q = _rope_tables(Sv, D_CQ)
        q_big = _apply_rope(q_big, sin_q[None, :, None, :], cos_q[None, :, None, :])
        sin_k, cos_k = _rope_tables(Lv, D_C)
        kv_r = _apply_rope(kv_c, sin_k[None], cos_k[None])
        q_r = jnp.einsum('bshq,hqr->bhsr', q_big, W_qr)
        k_r = jnp.einsum('bld,hdr->bhlr', kv_r, W_kr)
        scores = jnp.einsum('bhsr,bhlr->bhsl', q_r, k_r)
        attn = jax.nn.softmax(scores, axis=-1)
        ctx_c = jnp.einsum('bhsl,bld->bhsd', attn, kv_r)
        ctx_lat = jnp.einsum('bhsd,hkd->bhsk', ctx_c, w_kc_kv)
        ctx = ctx_lat.transpose(0, 2, 1, 3).reshape(Bv, Sv, H * K)
        return ctx @ Wo.T

    def _L1_ffn_ref(hidden_states, gate_w, expert_bias, shared_gate_w, shared_up_w, shared_down_w, experts_gate_up, experts_down):
        import jax, jax.numpy as jnp
        import numpy as np
        B, S, H = (1, 128, 256)
        F = 128
        E = 16
        K = 2
        NS = 1
        ROUTE_SCALE = 1.0
        b, s, h = hidden_states.shape
        x = hidden_states.reshape(-1, h)
        T = x.shape[0]
        router_logits = (x @ gate_w).astype(jnp.float32)
        scores = jax.nn.sigmoid(router_logits)
        _, selected = jax.lax.top_k(scores + expert_bias[None, :], K)
        top_scores = jnp.take_along_axis(scores, selected, axis=1)
        top_scores = top_scores / (top_scores.sum(-1, keepdims=True) + 1e-20)
        top_scores = top_scores * ROUTE_SCALE
        shared = jax.nn.silu(x @ shared_gate_w) * (x @ shared_up_w) @ shared_down_w
        comb = jnp.zeros((T, E), jnp.float32).at[jnp.arange(T)[:, None], selected].add(top_scores)
        routed = jnp.zeros_like(x)
        for e in range(E):
            gu = x @ experts_gate_up[e]
            g, u = jnp.split(gu, 2, axis=-1)
            routed = routed + comb[:, e:e + 1] * (jax.nn.silu(g) * u @ experts_down[e])
        return (shared + routed).reshape(b, s, h)
    x = x + jnp.tanh(g_xattn[0]) * _L0_xattn_ref(ctx_512, _layernorm(x, axis=-1), L0_xattn_Wq, L0_xattn_Wk, L0_xattn_gamma_raw)
    x = x + jnp.tanh(g_ffn[0]) * _L0_ffn_ref(_layernorm(x, axis=-1), L0_ffn_gate_weight, L0_ffn_gate_up_weights, L0_ffn_down_weights, L0_ffn_shared_gate_up, L0_ffn_shared_down)
    x = x + jnp.tanh(g_xattn[1]) * _L1_xattn_ref(_layernorm(x, axis=-1), ctx_512, L1_xattn_Wq, L1_xattn_w_kc_q, L1_xattn_w_kc_kv, L1_xattn_W_qr, L1_xattn_W_kr, L1_xattn_Wo)
    x = x + jnp.tanh(g_ffn[1]) * _L1_ffn_ref(_layernorm(x, axis=-1), L1_ffn_gate_w, L1_ffn_expert_bias, L1_ffn_shared_gate_w, L1_ffn_shared_up_w, L1_ffn_shared_down_w, L1_ffn_experts_gate_up, L1_ffn_experts_down)
    return x

_drawn_inputs = setup_inputs


def setup_inputs(seed=0):
    import zlib

    import numpy as np

    out = dict(_drawn_inputs(seed))
    spreads = {'g_ffn': (-1.0, 0.2), 'L1_ffn_expert_bias': (0.0, 0.1)}
    factors = {'L0_ffn_gate_weight': 6.825, 'L0_ffn_gate_up_weights': 3.824, 'L0_ffn_down_weights': 3.996}
    for name, (base, spread) in spreads.items():
        noise = np.random.default_rng([zlib.crc32(name.encode()), seed]).standard_normal(out[name].shape)
        drawn = base * np.exp(spread * noise) if base else spread * noise
        out[name] = jnp.asarray(drawn.astype(out[name].dtype))
    for name, factor in factors.items():
        out[name] = (out[name] * factor).astype(out[name].dtype)
    return out
```

```python
from contextlib import ExitStack

import numpy as np

import concourse.bass as bass
from concourse import mybir

F32 = mybir.dt.float32
F32R = mybir.dt.float32r
U32 = mybir.dt.uint32
ALU = mybir.AluOpType
ACT = mybir.ActivationFunctionType
AX_X = mybir.AxisListType.X

P = 128
B, S, D = 4, 256, 256
T = B * S
NT = T // P
KD = D // P
NCH = T // 512
C = 64
TOPK = int(S * 0.3)
EPS = 1e-5
E0, F0, FS0 = 8, 176, 352
R0 = E0 * F0 // P
N0 = R0 + (FS0 + P - 1) // P
E1, F1 = 16, 128
N1 = E1 + 1
H, KH, CQ, R = 16, 128, 192, 64
NPAIR = H // 2
JT = 2 * CQ // P
WC = 2 * 2 * P + D
PW = 2 * D + 2 * CQ + 2 * C + 2 * D
PR = 2 * 2 * CQ + 2 * C
NEG = -3.0e38


def build(nc, a, out):
    ctx = ExitStack()
    with ctx:
        def sb(name, shape, dt=F32):
            return ctx.enter_context(nc.sbuf_tensor(name, shape, dt))

        def sem(name):
            return ctx.enter_context(nc.semaphore(name))

        bank = [ctx.enter_context(nc.psum_tensor(f"bank{i}", [P, 512], F32)) for i in range(8)]

        x = sb("x", [P, NT, D])
        xn = sb("xn", [P, NT, D])
        xT_h = sb("xT_h", [P, KD, T], F32R)
        xT_l = sb("xT_l", [P, KD, T], F32R)
        ident = sb("ident", [P, P])
        iota = sb("iota", [P, E1])
        sel0 = sb("sel0", [E0, P])
        gates = sb("gates", [P, 5])
        tg = sb("tg", [P, 5])
        cc = sb("cc", [P, 4])
        bn = sb("bn", [P, NT, 6])
        mv = sb("mv", [P, NT, 2])
        rstd = sb("rstd", [P, NT])
        var = sb("var", [P, NT])
        root = sb("root", [P, NT])
        rg_raw = sb("rg_raw", [P, 2, KD, E1])
        rg_h = sb("rg_h", [P, 2, KD, E1], F32R)
        rg_l = sb("rg_l", [P, 2, KD, E1], F32R)
        bias1 = sb("bias1", [P, E1])
        sc = sb("sc", [P, NT, E1])
        sel = sb("sel", [P, NT, E1])
        oh = sb("oh", [P, NT, E1])
        oh2 = sb("oh2", [P, NT, E1])
        rmax = sb("rmax", [P, NT])
        rsum = sb("rsum", [P, NT])
        rinv = sb("rinv", [P, NT])
        top8 = sb("top8", [P, NT, 8])
        idx8 = sb("idx8", [P, NT, 8], U32)
        idxf = sb("idxf", [P, NT, 2])
        comb = sb("comb", [P, NT, N1])
        combT = sb("combT", [E0, T])

        class Seq:
            def __init__(self, eng, name):
                self.eng, self.sem, self.n = eng, sem(name), 0

            def did(self, ins):
                self.n += 1
                ins.then_inc(self.sem, 1)

            def link(self, ins):
                self.did(ins)
                self.eng.wait_ge(self.sem, self.n)

        s_ctx, s_wqk, s_x, s_const, s_rg, s_bias = (sem(n) for n in (
            "ctx_loaded", "wqk_loaded", "x_loaded", "const_loaded", "router_loaded", "bias_loaded"))
        s_out = sem("out_stored")
        s_gact = sem("gates_activated")
        s_rgh, s_rgl = sem("router_h_ready"), sem("router_l_ready")

        def layer_norm(dve, seq, n):
            for t in range(NT):
                seq.did(nc.vector.bn_stats(bn[:, t, :], x[:, t, :]))
            dve.wait_ge(seq.sem, seq.n)
            for t in range(NT):
                seq.did(nc.vector.bn_aggr(mv[:, t, :], bn[:, t, :]))
            dve.wait_ge(seq.sem, seq.n)
            nc.vector.tensor_scalar(var[:], mv[:, :, 1], EPS, None, ALU.add).then_inc(n.var, 1)
            dve.wait_ge(n.root, 1)
            seq.link(nc.vector.reciprocal(rstd[:], root[:]))
            seq.link(nc.vector.tensor_tensor(root[:], rstd[:], rstd[:], ALU.mult))
            seq.link(nc.vector.tensor_tensor(root[:], root[:], var[:], ALU.mult))
            seq.link(nc.vector.tensor_scalar(root[:], root[:], -0.5, 1.5, ALU.mult, ALU.add))
            seq.link(nc.vector.tensor_tensor(rstd[:], rstd[:], root[:], ALU.mult))
            for t in range(NT):
                ins = nc.vector.tensor_scalar(xn[:, t, :], x[:, t, :], mv[:, t, 0:1], rstd[:, t:t + 1],
                                              ALU.subtract, ALU.mult)
                if t % 2:
                    ins.then_inc(n.ln, 1)

        def norm_root(act, n):
            act.wait_ge(n.var, 1)
            nc.scalar.activation(root[:], var[:], ACT.Sqrt).then_inc(n.root, 1)

        class Norm:
            def __init__(self, name):
                self.var, self.root, self.ln, self.tr, self.h, self.l = (sem(f"{name}_{n}") for n in (
                    "variance_ready", "root_ready", "normed", "transposed", "xT_h_ready", "xT_l_ready"))

        def norm_pe(pe, n):
            for g in range(NT // 2):
                pe.wait_ge(n.ln, g + 1)
                if g >= 2:
                    pe.wait_ge(n.l, g - 1)
                for k in range(KD):
                    for j in range(2):
                        last = nc.tensor.matmul(bank[g % 2][:, k * 256 + j * P:k * 256 + (j + 1) * P],
                                                xn[:, 2 * g + j, k * P:(k + 1) * P], ident[:],
                                                start=True, stop=True, is_transpose=True)
                last.then_inc(n.tr, 1)

        def norm_act(act, n):
            for g in range(NT // 2):
                act.wait_ge(n.tr, g + 1)
                nc.scalar.activation(xT_h[:, :, g * 256:(g + 1) * 256],
                                     bank[g % 2][:].rearrange("p (k n) -> p k n", k=KD),
                                     ACT.Copy).then_inc(n.h, 1)

        def norm_dve_low(dve, n, g):
            dve.wait_ge(n.h, g + 1)
            nc.vector.tensor_tensor(xT_l[:, :, g * 256:(g + 1) * 256],
                                    bank[g % 2][:].rearrange("p (k n) -> p k n", k=KD),
                                    xT_h[:, :, g * 256:(g + 1) * 256], ALU.subtract).then_inc(n.l, 1)

        def router_pe(n, layer, ne, s_done, out_bank):
            for t in range(NT):
                parts = [(xh, rh, k) for xh, rh in ((xT_h, rg_h), (xT_h, rg_l), (xT_l, rg_h)) for k in range(KD)]
                for m, (xh, rh, k) in enumerate(parts):
                    last = nc.tensor.matmul(out_bank[:, t * ne:(t + 1) * ne], xh[:, k, t * P:(t + 1) * P],
                                            rh[:, layer, k, 0:ne], start=(m == 0), stop=(m == len(parts) - 1))
            last.then_inc(s_done, 1)

        def pick_two(seq, scores, choose, ne):
            for t in range(NT):
                seq.did(nc.vector.max(top8[:, t, :], choose[:, t, 0:ne]))
            seq.eng.wait_ge(seq.sem, seq.n)
            for t in range(NT):
                seq.did(nc.vector.max_index(idx8[:, t, :], top8[:, t, :], choose[:, t, 0:ne]))
            seq.eng.wait_ge(seq.sem, seq.n)
            seq.link(nc.vector.tensor_copy(idxf[:], idx8[:, :, 0:2]))
            io = iota[:, 0:ne].unsqueeze(1).broadcast_to([P, NT, ne])
            for o, j in ((oh, 0), (oh2, 1)):
                seq.did(nc.vector.tensor_tensor(o[:, :, 0:ne], io,
                                                idxf[:, :, j:j + 1].broadcast_to([P, NT, ne]), ALU.is_equal))
            seq.eng.wait_ge(seq.sem, seq.n)
            seq.link(nc.vector.tensor_tensor(oh[:, :, 0:ne], oh[:, :, 0:ne], oh2[:, :, 0:ne], ALU.add))
            seq.link(nc.vector.tensor_tensor(oh[:, :, 0:ne], oh[:, :, 0:ne], scores[:, :, 0:ne], ALU.mult))

        norms = [Norm("l0_att"), Norm("l0_ffn"), Norm("l1_att"), Norm("l1_ffn")]

        ctx_n = sb("ctx_n", [P, NT, C])
        wqk = sb("wqk", [C, 2, C])
        with nc.Block() as block:
            @block.sync
            def _(sp):
                sp.dma_start(ctx_n[:], a["ctx"]).then_inc(s_ctx, 16)
                sp.dma_start(wqk[:], a["wqk"]).then_inc(s_wqk, 16)
                sp.dma_start(ident[:], a["ident"]).then_inc(s_const, 16)
                sp.dma_start(gates[:], a["gates"].partition_broadcast(P)).then_inc(s_const, 16)
                sp.dma_start(iota[:], a["iota"].partition_broadcast(P)).then_inc(s_const, 16)
                sp.dma_start(sel0[:], a["sel0"]).then_inc(s_const, 16)
                sp.dma_start(x[:], a["x"]).then_inc(s_x, 16)
                sp.dma_start(rg_raw[:], a["router"]).then_inc(s_rg, 16)
                sp.dma_start(bias1[:], a["bias1"].partition_broadcast(P)).then_inc(s_bias, 16)

        with ExitStack() as st:
            def lsb(name, shape, dt=F32):
                return st.enter_context(nc.sbuf_tensor(name, shape, dt))
            ctxT = lsb("ctxT", [C, T])
            bmat = lsb("bmat", [C, C])
            pT = lsb("pT", [C, T])
            sim = lsb("sim", [P, NT, S])
            sig = lsb("sig", [P, NT, S])
            left = lsb("left", [P, 2, S])
            best = lsb("best", [P, 2, 8])
            adj = lsb("adj", [P, NT, S])

            s_ct, s_ctc = sem("ctx_transposed"), sem("ctxT_ready")
            s_bm, s_bmc, s_pt, s_ptc = sem("bmat_done"), sem("bmat_ready"), sem("pT_done"), sem("pT_ready")
            s_sim, s_simc, s_sig = sem("sim_done"), sem("sim_ready"), sem("sigmoid_ready")
            s_adj, s_adjT, s_upd = sem("adj_ready"), sem("adj_transposed"), sem("l0_att_updated")
            ln0 = norms[0]

            with nc.Block() as block:
                @block.tensor
                def _(pe):
                    pe.wait_ge(s_const, 64)
                    pe.wait_ge(s_ctx, 16)
                    for t in range(NT):
                        last = nc.tensor.matmul(bank[t // 4][0:C, (t % 4) * P:(t % 4 + 1) * P], ctx_n[:, t, :],
                                                ident[:], start=True, stop=True, is_transpose=True)
                        if t % 4 == 3:
                            last.then_inc(s_ct, 1)
                    pe.wait_ge(s_wqk, 16)
                    nc.tensor.matmul(bank[2][0:C, 0:C], wqk[:, 0, :], wqk[:, 1, :],
                                     start=True, stop=True).then_inc(s_bm, 1)
                    pe.wait_ge(s_bmc, 1)
                    for c in range(NCH):
                        pe.wait_ge(s_ctc, c + 1)
                        nc.tensor.matmul(bank[3 + c][0:C, :], bmat[:], ctxT[:, c * 512:(c + 1) * 512],
                                         start=True, stop=True).then_inc(s_pt, 1)
                    for t in range(NT):
                        pe.wait_ge(s_ptc, t // 4 + 1)
                        bk = bank[5 + (t // 2) % 2]
                        if t >= 4 and t % 2 == 0:
                            pe.wait_ge(s_simc, t // 2 - 1)
                        last = nc.tensor.matmul(bk[:, (t % 2) * S:(t % 2 + 1) * S], pT[:, t * P:(t + 1) * P],
                                                ctxT[:, (t // 2) * S:(t // 2 + 1) * S], start=True, stop=True)
                        if t % 2:
                            last.then_inc(s_sim, 1)
                    for b in range(B):
                        pe.wait_ge(s_adj, b + 1)
                        if b >= 2:
                            pe.wait_ge(s_upd, 2 * (b - 1))
                        for c in range(2):
                            for r in range(2):
                                last = nc.tensor.matmul(bank[b % 2][:, c * S + r * P:c * S + (r + 1) * P],
                                                        adj[:, 2 * b + r, c * P:(c + 1) * P], ident[:],
                                                        start=True, stop=True, is_transpose=True)
                        last.then_inc(s_adjT, 1)

                @block.scalar
                def _(act):
                    for c in range(NCH):
                        act.wait_ge(s_ct, c + 1)
                        nc.scalar.activation(ctxT[:, c * 512:(c + 1) * 512], bank[c][0:C, :],
                                             ACT.Copy).then_inc(s_ctc, 1)
                    act.wait_ge(s_bm, 1)
                    nc.scalar.activation(bmat[:], bank[2][0:C, 0:C], ACT.Copy).then_inc(s_bmc, 1)
                    for c in range(NCH):
                        act.wait_ge(s_pt, c + 1)
                        nc.scalar.activation(pT[:, c * 512:(c + 1) * 512], bank[3 + c][0:C, :],
                                             ACT.Copy).then_inc(s_ptc, 1)
                    for g in range(NT // 2):
                        act.wait_ge(s_sim, g + 1)
                        nc.scalar.activation(sim[:, 2 * g:2 * g + 2, :],
                                             bank[5 + g % 2][:].rearrange("p (t n) -> p t n", t=2),
                                             ACT.Copy).then_inc(s_simc, 1)
                    norm_root(act, ln0)
                    act.wait_ge(s_const, 64)
                    nc.scalar.activation(tg[:, 0:4], gates[:, 0:4], ACT.Tanh).then_inc(s_gact, 1)
                    nc.scalar.activation(tg[:, 4:5], gates[:, 4:5], ACT.Sigmoid).then_inc(s_gact, 1)
                    act.wait_ge(s_simc, NT // 2)
                    for g in range(NT // 2):
                        nc.scalar.activation(sig[:, 2 * g:2 * g + 2, :], sim[:, 2 * g:2 * g + 2, :],
                                             ACT.Sigmoid, scale=1.0 / 16.0).then_inc(s_sig, 1)
                    act.wait_ge(s_rg, 16)
                    nc.scalar.activation(rg_h[:], rg_raw[:], ACT.Copy).then_inc(s_rgh, 1)

                @block.gpsimd
                def _(pool):
                    pool.wait_ge(s_rgh, 1)
                    nc.gpsimd.tensor_tensor(rg_l[:], rg_raw[:], rg_h[:], ALU.subtract).then_inc(s_rgl, 1)

                @block.vector
                def _(dve):
                    seq = Seq(dve, "l0_att_vector_step")
                    dve.wait_ge(s_x, 16)
                    layer_norm(dve, seq, ln0)
                    dve.wait_ge(s_gact, 2)
                    seq.link(nc.vector.tensor_tensor(cc[:, 0:1], tg[:, 0:1], tg[:, 4:5], ALU.mult))
                    seq.did(nc.vector.tensor_tensor(cc[:, 1:2], tg[:, 0:1], cc[:, 0:1], ALU.subtract))
                    seq.link(nc.vector.tensor_scalar(cc[:, 2:3], cc[:, 0:1], 0.5, None, ALU.mult))
                    dve.wait_ge(ln0.ln, NT // 2)
                    for g in range(NT // 2):
                        pair = (2 * g, 2 * g + 1)
                        dve.wait_ge(s_simc, g + 1)
                        rounds = (TOPK + 7) // 8
                        for r in range(rounds):
                            for j, t in enumerate(pair):
                                src = sim[:, t, :] if r == 0 else left[:, j, :]
                                if r:
                                    dve.wait_ge(seq.sem, seq.n - 1)
                                seq.did(nc.vector.max(best[:, j, :], src))
                            if r < rounds - 1:
                                for j, t in enumerate(pair):
                                    src = sim[:, t, :] if r == 0 else left[:, j, :]
                                    dve.wait_ge(seq.sem, seq.n - 1)
                                    seq.did(nc.vector.match_replace(left[:, j, :], best[:, j, :], src, NEG))
                        dve.wait_ge(s_sig, g + 1)
                        dve.wait_ge(seq.sem, seq.n)
                        kth = (TOPK - 1) % 8
                        for j, t in enumerate(pair):
                            last = nc.vector.scalar_tensor_tensor(
                                out=adj[:, t, :], in0=sim[:, t, :], scalar=best[:, j, kth:kth + 1],
                                in1=sig[:, t, :], op0=ALU.is_ge, op1=ALU.mult)
                        last.then_inc(s_adj, 1)
                        for t in pair:
                            seq.did(nc.vector.scalar_tensor_tensor(
                                out=x[:, t, :], in0=xn[:, t, :], scalar=cc[:, 1:2], in1=x[:, t, :],
                                op0=ALU.mult, op1=ALU.add))
                        dve.wait_ge(s_adj, g + 1)
                        dve.wait_ge(seq.sem, seq.n)
                        for t in pair:
                            seq.did(nc.vector.scalar_tensor_tensor(
                                out=x[:, t, :], in0=adj[:, t, :], scalar=cc[:, 2:3], in1=x[:, t, :],
                                op0=ALU.mult, op1=ALU.add))
                        dve.wait_ge(seq.sem, seq.n)
                        dve.wait_ge(s_adjT, g + 1)
                        for j, t in enumerate(pair):
                            nc.vector.scalar_tensor_tensor(
                                out=x[:, t, :], in0=bank[g % 2][:, j * S:(j + 1) * S], scalar=cc[:, 2:3],
                                in1=x[:, t, :], op0=ALU.mult, op1=ALU.add).then_inc(s_upd, 1)

        def ffn(name, norm, n, n_loop, weights, layer, ne, route_dve, scale_rows, n_routed, route_act, x_ready):
            with ExitStack() as st:
                def lsb(nm, shape, dt=F32):
                    return st.enter_context(nc.sbuf_tensor(f"{name}_{nm}", shape, dt))
                raw = [lsb(f"raw{i}", [P, WC]) for i in range(2)]
                w_h = [lsb(f"w_h{i}", [P, WC], F32R) for i in range(2)]
                w_l = [lsb(f"w_l{i}", [P, WC], F32R) for i in range(2)]
                silu = [lsb(f"silu{c}", [P, 512]) for c in range(2)]
                hid = [lsb(f"hid{c}", [P, 512]) for c in range(2)]
                hid_h = [lsb(f"hid_h{c}", [P, 512], F32R) for c in range(2)]
                hid_l = [lsb(f"hid_l{c}", [P, 512], F32R) for c in range(2)]
                rows = lsb("rows", [P, T]) if scale_rows else None

                def lsem(nm):
                    return sem(f"{name}_{nm}")
                s_raw = [lsem(f"raw{i}_loaded") for i in range(2)]
                s_wgh, s_wgl, s_wdh, s_wdl = (lsem(nm) for nm in (
                    "gateup_h_ready", "gateup_l_ready", "down_h_ready", "down_l_ready"))
                s_gu, s_silu, s_hid, s_hh, s_hl = (lsem(nm) for nm in (
                    "gateup_done", "silu_ready", "hidden_ready", "hidden_h_ready", "hidden_l_ready"))
                s_down, s_rowm = lsem("down_done"), lsem("hidden_unscaled")
                s_acc = [lsem(f"added{c}") for c in range(2)]
                s_logit, s_ract, s_comb = lsem("logits_done"), lsem("router_activated"), lsem("comb_ready")
                s_cT, s_cTc, s_row, s_rowc = (lsem(nm) for nm in (
                    "comb_transposed", "combT_ready", "rows_done", "rows_ready"))
                GU = 2 * 2 * P

                def both(eng, body, tail):
                    with eng.Fori(0, n_loop // 2) as ii:
                        for b in range(2):
                            body(ii * 2 + b, b, False)
                    for e in range(n_loop, n - 1):
                        body(e, e % 2, True)
                    tail(n - 1)

                with nc.Block() as block:
                    @block.sync
                    def _(sp):
                        for e in range(2):
                            sp.dma_start(raw[e][:], weights[e]).then_inc(s_raw[e], 16)

                        def load(e, b, static):
                            if static and e + 2 >= n:
                                return
                            sp.wait_ge(s_wdl, e + 1)
                            sp.dma_start(raw[b][:], weights[e + 2]).then_inc(s_raw[b], 16)
                        both(sp, load, lambda e: None)

                    @block.gpsimd
                    def _(pool):
                        def split(e, b, turn):
                            pool.wait_ge(s_wgh, e + 1)
                            nc.gpsimd.tensor_tensor(w_l[b][:, 0:GU], raw[b][:, 0:GU], w_h[b][:, 0:GU],
                                                    ALU.subtract).then_inc(s_wgl, 1)
                            pool.wait_ge(s_wdh, e + 1)
                            nc.gpsimd.tensor_tensor(w_l[b][:, GU:WC], raw[b][:, GU:WC], w_h[b][:, GU:WC],
                                                    ALU.subtract).then_inc(s_wdl, 1)
                        split(0, 0, 1)
                        both(pool, lambda e, b, static: split(e + 1, 1 - b, None), lambda e: None)

                    @block.scalar
                    def _(act):
                        def split_gateup(e, b, loads):
                            act.wait_ge(s_raw[b], loads * 16)
                            nc.scalar.activation(w_h[b][:, 0:GU], raw[b][:, 0:GU], ACT.Copy).then_inc(s_wgh, 1)

                        def split_down(e, b):
                            nc.scalar.activation(w_h[b][:, GU:WC], raw[b][:, GU:WC], ACT.Copy).then_inc(s_wdh, 1)

                        def hidden(e, c):
                            act.wait_ge(s_gu, e * 2 + c + 1)
                            nc.scalar.activation(silu[c][:], bank[2 * c][:], ACT.Silu).then_inc(s_silu, 1)

                        def high(e, c):
                            act.wait_ge(s_hid, e * 2 + c + 1)
                            nc.scalar.activation(hid_h[c][:], hid[c][:], ACT.Copy).then_inc(s_hh, 1)

                        split_gateup(0, 0, 1)
                        split_down(0, 0)
                        norm_root(act, norm)
                        norm_act(act, norm)
                        route_act(act, s_logit, s_ract)
                        if scale_rows:
                            for c in range(NCH):
                                act.wait_ge(s_cT, c + 1)
                                nc.scalar.activation(combT[:, c * 512:(c + 1) * 512], bank[6 + c][0:E0, :],
                                                     ACT.Copy).then_inc(s_cTc, 1)
                            for c in range(NCH):
                                act.wait_ge(s_row, c + 1)
                                nc.scalar.activation(rows[:, c * 512:(c + 1) * 512], bank[4 + c][:],
                                                     ACT.Copy).then_inc(s_rowc, 1)
                        hidden(0, 0)
                        high(0, 0)

                        def body(e, b, loads):
                            split_gateup(e + 1, 1 - b, loads)
                            hidden(e, 1)
                            high(e, 1)
                            act.wait_ge(s_acc[1], e + 1)
                            split_down(e + 1, 1 - b)
                            hidden(e + 1, 0)
                            high(e + 1, 0)

                        with act.Fori(0, n_loop // 2) as ii:
                            for b in range(2):
                                body(ii * 2 + b, b, ii + (b + 1))
                        for e in range(n_loop, n - 1):
                            body(e, e % 2, (e + 1) // 2 + 1)
                        hidden(n - 1, 1)
                        high(n - 1, 1)

                    @block.vector
                    def _(dve):
                        seq = Seq(dve, f"{name}_vector_step")
                        for c in range(NCH):
                            dve.sem_inc(s_acc[c], 1)
                        layer_norm(dve, seq, norm)
                        for g in range(NT // 2):
                            norm_dve_low(dve, norm, g)
                        route_dve(dve, seq, s_logit, s_ract, s_comb)

                        def hidden(e, c, shared):
                            dve.wait_ge(s_silu, e * 2 + c + 1)
                            if scale_rows and not shared:
                                nc.vector.tensor_tensor(hid[c][:], silu[c][:], bank[2 * c + 1][:],
                                                        ALU.mult).then_inc(s_rowm, 1)
                                dve.wait_ge(s_rowm, e * 2 + c + 1)
                                nc.vector.tensor_tensor(hid[c][:], hid[c][:], rows[:, c * 512:(c + 1) * 512],
                                                        ALU.mult).then_inc(s_hid, 1)
                            elif scale_rows:
                                nc.vector.scalar_tensor_tensor(
                                    out=hid[c][:], in0=silu[c][:], scalar=tg[:, 2 + layer:3 + layer],
                                    in1=bank[2 * c + 1][:], op0=ALU.mult, op1=ALU.mult).then_inc(s_hid, 1)
                            else:
                                nc.vector.tensor_tensor(hid[c][:], silu[c][:], bank[2 * c + 1][:],
                                                        ALU.mult).then_inc(s_hid, 1)

                        def low(e, c):
                            dve.wait_ge(s_hh, e * 2 + c + 1)
                            nc.vector.tensor_tensor(hid_l[c][:], hid[c][:], hid_h[c][:],
                                                    ALU.subtract).then_inc(s_hl, 1)

                        def add(e, c):
                            dve.wait_ge(s_down, e * 2 + c + 1)
                            for j in range(2):
                                t = 4 * c + 2 * j
                                if scale_rows:
                                    last = nc.vector.tensor_tensor(
                                        x[:, t:t + 2, :], bank[4 + 2 * c + j][:].rearrange("p (t d) -> p t d", t=2),
                                        x[:, t:t + 2, :], ALU.add)
                                else:
                                    for i in range(2):
                                        col = comb[:, t + i, e:e + 1] if isinstance(e, int) else \
                                            comb[:, t + i, bass.ds(e, 1)]
                                        last = nc.vector.scalar_tensor_tensor(
                                            out=x[:, t + i, :], in0=bank[4 + 2 * c + j][:, i * D:(i + 1) * D],
                                            scalar=col, in1=x[:, t + i, :], op0=ALU.mult, op1=ALU.add)
                            last.then_inc(s_acc[c], 1)

                        if scale_rows:
                            dve.wait_ge(s_rowc, NCH)
                        hidden(0, 0, False)
                        low(0, 0)

                        def body(e, b, static):
                            hidden(e, 1, static and e >= n_routed)
                            add(e, 0)
                            low(e, 1)
                            hidden(e + 1, 0, static and e + 1 >= n_routed)
                            add(e, 1)
                            low(e + 1, 0)

                        def tail(e):
                            hidden(e, 1, e >= n_routed)
                            add(e, 0)
                            low(e, 1)
                            add(e, 1)
                        both(dve, body, tail)
                        dve.wait_ge(s_acc[0], n + 1)
                        dve.wait_ge(s_acc[1], n + 1)

                    @block.tensor
                    def _(pe):
                        def gateup(e, b, c):
                            pe.wait_ge(s_wgl, e + 1)
                            for g in range(2):
                                m = 0
                                for wp, xp in ((w_h, xT_h), (w_h, xT_l), (w_l, xT_h)):
                                    for k in range(KD):
                                        last = nc.tensor.matmul(
                                            bank[2 * c + g][:], wp[b][:, (2 * k + g) * P:(2 * k + g + 1) * P],
                                            xp[:, k, c * 512:(c + 1) * 512], start=(m == 0), stop=(m == 5))
                                        m += 1
                            last.then_inc(s_gu, 1)

                        def down(e, b, c):
                            pe.wait_ge(s_hl, e * 2 + c + 1)
                            pe.wait_ge(s_wdl, e + 1)
                            pe.wait_ge(s_acc[c], e + 1)
                            for t in range(4):
                                bk = bank[4 + 2 * c + t // 2]
                                for m, (hp, wp) in enumerate(((hid_h, w_h), (hid_h, w_l), (hid_l, w_h))):
                                    last = nc.tensor.matmul(bk[:, (t % 2) * D:(t % 2 + 1) * D],
                                                            hp[c][:, t * P:(t + 1) * P], wp[b][:, GU:WC],
                                                            start=(m == 0), stop=(m == 2))
                            last.then_inc(s_down, 1)

                        norm_pe(pe, norm)
                        pe.wait_ge(norm.l, NT // 2)
                        pe.wait_ge(s_rgl, 1)
                        router_pe(norm, layer, ne, s_logit, bank[7])
                        gateup(0, 0, 0)
                        if scale_rows:
                            pe.wait_ge(s_comb, 1)
                            for c in range(NCH):
                                for j in range(4):
                                    last = nc.tensor.matmul(bank[6 + c][0:E0, j * P:(j + 1) * P],
                                                            comb[:, 4 * c + j, 0:E0], ident[:],
                                                            start=True, stop=True, is_transpose=True)
                                last.then_inc(s_cT, 1)
                            for c in range(NCH):
                                pe.wait_ge(s_cTc, c + 1)
                                nc.tensor.matmul(bank[4 + c][:], sel0[:], combT[:, c * 512:(c + 1) * 512],
                                                 start=True, stop=True).then_inc(s_row, 1)
                            pe.wait_ge(s_rowc, NCH)

                        def body(e, b, static):
                            gateup(e, b, 1)
                            down(e, b, 0)
                            gateup(e + 1, 1 - b, 0)
                            down(e, b, 1)

                        def tail(e):
                            gateup(e, e % 2, 1)
                            down(e, e % 2, 0)
                            down(e, e % 2, 1)
                        both(pe, body, tail)

        s_r0 = sem("l0_scores_shifted")

        def route0_act(act, s_logit, s_ract):
            act.wait_ge(s_r0, 1)
            nc.scalar.activation(sc[:, :, 0:E0], sel[:, :, 0:E0], ACT.Exp).then_inc(s_ract, 1)

        def route0_dve(dve, seq, s_logit, s_ract, s_comb):
            dve.wait_ge(s_logit, 1)
            lg = bank[7][:, 0:NT * E0].rearrange("p (t e) -> p t e", e=E0)
            seq.link(nc.vector.tensor_reduce(rmax[:], lg, AX_X, ALU.max))
            nc.vector.tensor_tensor(sel[:, :, 0:E0], lg, rmax[:].unsqueeze(2).broadcast_to([P, NT, E0]),
                                    ALU.subtract).then_inc(s_r0, 1)
            dve.wait_ge(s_ract, 1)
            seq.link(nc.vector.tensor_reduce(rsum[:], sc[:, :, 0:E0], AX_X, ALU.add))
            seq.link(nc.vector.reciprocal(rinv[:], rsum[:]))
            seq.link(nc.vector.tensor_tensor(sc[:, :, 0:E0], sc[:, :, 0:E0],
                                             rinv[:].unsqueeze(2).broadcast_to([P, NT, E0]), ALU.mult))
            pick_two(seq, sc, sc, E0)
            nc.vector.tensor_scalar(comb[:, :, 0:E0], oh[:, :, 0:E0], tg[:, 2:3], None,
                                    ALU.mult).then_inc(s_comb, 1)

        ffn("l0_ffn", norms[1], N0, 10, a["w_ffn0"], 0, E0, route0_dve, True, R0, route0_act, None)

        with ExitStack() as st:
            def lsb(name, shape, dt=F32):
                return st.enter_context(nc.sbuf_tensor(name, shape, dt))
            cosq = lsb("cosq", [P, JT, S])
            sinq = lsb("sinq", [P, JT, S])
            trigk = lsb("trigk", [P, 2, 2, C])
            kvc = lsb("kvc", [P, NT, C])
            kvs = lsb("kvs", [P, NT, C])
            kv = lsb("kv", [P, NT, 2 * C])
            ks_h = lsb("ks_h", [P, T], F32R)
            ks_l = lsb("ks_l", [P, T], F32R)
            pw = [lsb(f"pair_w{i}", [P, PW]) for i in range(2)]
            pr = [lsb(f"pair_r{i}", [R, PR]) for i in range(2)]
            m_h = lsb("m_h", [P, KD, 2 * CQ], F32R)
            m_l = lsb("m_l", [P, KD, 2 * CQ], F32R)
            gt = lsb("gt", [P, 2 * JT, P])
            f_h = [lsb(f"f_h{i}", [P, D], F32R) for i in range(2)]
            f_l = [lsb(f"f_l{i}", [P, D], F32R) for i in range(2)]
            qc = [lsb(f"qc{i}", [P, 512]) for i in range(2)]
            qn = [lsb(f"qn{i}", [P, 512]) for i in range(2)]
            qs = [[lsb(f"qs{i}_{h}", [P, T], F32R) for h in range(2)] for i in range(2)]
            negm = lsb("negm", [P, 2, 2])
            den = lsb("den", [P, 2, 2])
            rden = lsb("rden", [P, 2, 2])
            ex = [lsb(f"ex{i}", [P, 2, S]) for i in range(2)]
            pn = [lsb(f"pn{i}", [P, 2, S]) for i in range(2)]
            pT2 = [lsb(f"probsT{i}", [P, 2, 2, S]) for i in range(2)]
            c_h = [lsb(f"c_h{i}", [P, S], F32R) for i in range(2)]
            c_l = [lsb(f"c_l{i}", [P, S], F32R) for i in range(2)]

            def wq_of(b, h, k):
                return pw[b][:, h * D + k * P:h * D + (k + 1) * P]

            def wkq_of(b, h):
                return pw[b][:, 2 * D + h * CQ:2 * D + (h + 1) * CQ]

            def wkv_of(b, h):
                o = 2 * D + 2 * CQ + h * C
                return pw[b][:, o:o + C]

            def wo_of(b, h):
                o = 2 * D + 2 * CQ + 2 * C + h * D
                return pw[b][:, o:o + D]

            s_trig, s_trigk = sem("ropeq_loaded"), sem("ropek_loaded")
            s_pw = [sem(f"pair_w{i}_loaded") for i in range(2)]
            s_kv, s_kvT, s_ksh, s_ksl, s_zero = (sem(n) for n in (
                "kv_roped", "kv_transposed", "ks_h_ready", "ks_l_ready", "gt_zeroed"))
            s_m, s_mh, s_ml, s_g, s_gc, s_fh, s_fl = (sem(n) for n in (
                "m_done", "m_h_ready", "m_l_ready", "g_f_done", "g_ready", "f_h_ready", "f_l_ready"))
            s_q, s_cs, s_rp, s_qh, s_ql = (sem(n) for n in (
                "q_done", "q_cos_sin_ready", "q_rope_done", "qs_h_ready", "qs_l_ready"))
            s_sc, s_nm, s_ex, s_pn, s_tr, s_ev = (sem(n) for n in (
                "scores_done", "max_ready", "exp_ready", "probs_ready", "probs_transposed", "probsT_ready"))
            s_rd = sem("inverse_sum_ready")
            s_av, s_ch, s_cl, s_y, s_xa = (sem(n) for n in (
                "values_done", "values_h_ready", "values_l_ready", "projected", "att_added"))
            norm = norms[2]

            Q_AT = {0: 0, 1: 1, 3: 2, 4: 3, 6: 4, 7: 5}
            SLOTS = 11
            NU = NT

            def run_pairs(eng, slot, pre):
                pre()
                for n in range(SLOTS):
                    slot(n, 0, 0, 0, False, True, 1)
                with eng.Fori(0, 3) as ii:
                    for h in range(2):
                        for n in range(SLOTS):
                            slot(n, ii * 2 + (1 + h), (1 + h) % 2, ii, True, True, ii + 2)
                for n in range(SLOTS):
                    slot(n, NPAIR - 1, (NPAIR - 1) % 2, None, True, True, None)
                for n in range(SLOTS):
                    slot(n, NPAIR, NPAIR % 2, None, True, False, None)

            with nc.Block() as block:
                @block.sync
                def _(sp):
                    sp.dma_start(trigk[:], a["trigk"]).then_inc(s_trigk, 16)
                    for i in range(2):
                        sp.dma_start(pw[i][:], a["pair_w"][i]).then_inc(s_pw[i], 16)
                        sp.dma_start(pr[i][:], a["pair_r"][i]).then_inc(s_pw[i], 16)
                        if i == 0:
                            sp.dma_start(cosq[:], a["cosq"]).then_inc(s_trig, 16)
                            sp.dma_start(sinq[:], a["sinq"]).then_inc(s_trig, 16)
                    with sp.Fori(0, (NPAIR - 2) // 2) as ii:
                        for b in range(2):
                            sp.wait_ge(s_g, ii * 2 + b + 1)
                            sp.dma_start(pw[b][:], a["pair_w"][ii * 2 + b + 2]).then_inc(s_pw[b], 16)
                            sp.dma_start(pr[b][:], a["pair_r"][ii * 2 + b + 2]).then_inc(s_pw[b], 16)

                @block.gpsimd
                def _(pool):
                    nc.gpsimd.memset(gt[:], 0.0).then_inc(s_zero, 1)

                @block.tensor
                def _(pe):
                    def fold_m(i, b, loads):
                        pe.wait_ge(s_pw[b], loads * 32)
                        if not (isinstance(i, int) and i == 0):
                            pe.wait_ge(s_cs, i * 6)
                        for k in range(KD):
                            for h in range(2):
                                last = nc.tensor.matmul(bank[k][:, h * CQ:(h + 1) * CQ], wq_of(b, h, k),
                                                        wkq_of(b, h), start=True, stop=True)
                        last.then_inc(s_m, 1)

                    def fold_g(i, b):
                        pe.wait_ge(s_ml, i + 1)
                        for j in range(2 * JT):
                            bk, o = (bank[0], j * P) if j < 4 else (bank[1], (j - 4) * P)
                            src = (j % 2) * 2 * CQ + (j // 2) * P
                            nc.tensor.matmul(bk[:, o:o + P], pr[b][:, src:src + P],
                                             pr[b][:, 4 * CQ:4 * CQ + 2 * C], start=True, stop=True)
                        for h in range(2):
                            last = nc.tensor.matmul(bank[1][h * C:(h + 1) * C, D:2 * D], wkv_of(b, h),
                                                    wo_of(b, h), start=True, stop=True, skip_group_check=True)
                        last.then_inc(s_g, 1)

                    def q_step(i, n):
                        c, j = n // JT, n % JT
                        if n == 0:
                            pe.wait_ge(s_gc, i + 1)
                        if n == 1:
                            pe.wait_ge(s_fl, i + 1)
                        if n >= 2:
                            pe.wait_ge(s_cs, i * 6 + (n - 1))
                        m = 0
                        for wp, xp in ((m_h, xT_h), (m_h, xT_l), (m_l, xT_h)):
                            for k in range(KD):
                                last = nc.tensor.matmul(bank[n % 2][:], wp[:, k, j * P:(j + 1) * P],
                                                        xp[:, k, c * 512:(c + 1) * 512],
                                                        start=(m == 0), stop=(m == 5))
                                m += 1
                        last.then_inc(s_q, 1)

                    def rope_step(i, n):
                        c, j = n // JT, n % JT
                        pe.wait_ge(s_cs, i * 6 + (n + 1))
                        if j == 0 and not (isinstance(i, int) and i + c == 0):
                            pe.wait_ge(s_ql, i * 2 + c)
                        nc.tensor.matmul(bank[2][:], gt[:, 2 * j, :], qc[n % 2][:], start=(j == 0), stop=False)
                        nc.tensor.matmul(bank[2][:], gt[:, 2 * j + 1, :], qn[n % 2][:],
                                         start=False, stop=(j == JT - 1)).then_inc(s_rp, 1)

                    def scores(j, jb, u):
                        if u % 4 == 0:
                            pe.wait_ge(s_ql, j * 2 + (u // 4 + 1))
                        keys = slice((u // 2) * S, (u // 2 + 1) * S)
                        for h in range(2):
                            o = bank[4 + u % 2][:, h * S:(h + 1) * S]
                            q = qs[jb][h][:, u * P:(u + 1) * P]
                            nc.tensor.matmul(o, q, ks_h[:, keys], start=True, stop=False)
                            last = nc.tensor.matmul(o, q, ks_l[:, keys], start=False, stop=True)
                        last.then_inc(s_sc, 1)

                    def transpose_probs(j, u):
                        pe.wait_ge(s_pn, j * 8 + (u + 1))
                        pe.wait_ge(s_ev, j * 8 + (u + 1))
                        for h in range(2):
                            for k in range(2):
                                last = nc.tensor.matmul(bank[6][:, (2 * h + k) * P:(2 * h + k + 1) * P],
                                                        pn[u % 2][:, h, k * P:(k + 1) * P], ident[:],
                                                        start=True, stop=True, is_transpose=True)
                        last.then_inc(s_tr, 1)

                    def values(j, b):
                        pe.wait_ge(s_ev, j * 8 + (2 * b + 3))
                        pe.wait_ge(s_cl, j * 4 + (b + 1))
                        for k in range(2):
                            for h in range(2):
                                last = nc.tensor.matmul(bank[7][h * C:(h + 1) * C, 0:S],
                                                        kv[:, 2 * b + k, 0:C], pT2[b % 2][:, h, k, :],
                                                        start=(k == 0), stop=(k == 1), skip_group_check=True)
                        last.then_inc(s_av, 1)

                    def project(j, jb, b):
                        pe.wait_ge(s_cl, j * 4 + (b + 2))
                        pe.wait_ge(s_xa, j * 4 + (b + 1))
                        if b == 0:
                            pe.wait_ge(s_fl, j + 1)
                        for t in range(2):
                            for m, (cp, fp) in enumerate(((c_h, f_h), (c_h, f_l), (c_l, f_h))):
                                last = nc.tensor.matmul(bank[3][:, t * D:(t + 1) * D],
                                                        cp[b % 2][:, t * P:(t + 1) * P], fp[jb][:],
                                                        start=(m == 0), stop=(m == 2))
                        last.then_inc(s_y, 1)

                    def slot(n, i, b, ii, do_s, do_q, loads):
                        j, jb = i - 1, 1 - b
                        if do_s and n < NU:
                            scores(j, jb, n)
                        if do_q and n in Q_AT:
                            q_step(i, Q_AT[n])
                            if Q_AT[n]:
                                rope_step(i, Q_AT[n] - 1)
                        if do_s and 1 <= n <= NU:
                            transpose_probs(j, n - 1)
                        if do_q and n == 8:
                            rope_step(i, 5)
                            if loads is not None:
                                fold_m(i + 1, 1 - b, loads)
                        if do_s and n >= 3 and n % 2:
                            values(j, (n - 3) // 2)
                        if do_q and n == 9 and loads is not None:
                            fold_g(i + 1, 1 - b)
                        if do_s and n >= 4 and n % 2 == 0:
                            project(j, jb, (n - 4) // 2)

                    def pre():
                        norm_pe(pe, norm)
                        pe.wait_ge(s_kv, 1)
                        for t in range(NT):
                            last = nc.tensor.matmul(bank[4 + t // 4][:, (t % 4) * P:(t % 4 + 1) * P],
                                                    kv[:, t, :], ident[:], start=True, stop=True,
                                                    is_transpose=True)
                        last.then_inc(s_kvT, 1)
                        pe.wait_ge(norm.l, NT // 2)
                        fold_m(0, 0, 1)
                        fold_g(0, 0)
                        pe.wait_ge(s_ksl, 1)
                    run_pairs(pe, slot, pre)

                @block.scalar
                def _(act):
                    def m_high(i):
                        act.wait_ge(s_m, i + 1)
                        for k in range(KD):
                            last = nc.scalar.activation(m_h[:, k, :], bank[k][:, 0:2 * CQ], ACT.Copy)
                        last.then_inc(s_mh, 1)

                    def g_copy(i):
                        act.wait_ge(s_g, i + 1)
                        b0 = bank[0][:].rearrange("p (j n) -> p j n", n=P)
                        b1 = bank[1][:].rearrange("p (j n) -> p j n", n=P)
                        nc.scalar.activation(gt[:, 0:2, 0:C], b0[:, 0:2, 0:C], ACT.Copy)
                        nc.scalar.activation(gt[0:C, 2:4, 0:C], b0[0:C, 2:4, 0:C], ACT.Copy)
                        nc.scalar.activation(gt[C:P, 2:4, C:P], b0[C:P, 2:4, C:P], ACT.Copy)
                        nc.scalar.activation(gt[:, 4:6, C:P], b1[:, 0:2, C:P], ACT.Copy).then_inc(s_gc, 1)

                    def f_high(i, b):
                        nc.scalar.activation(f_h[b][:], bank[1][:, D:2 * D], ACT.Copy).then_inc(s_fh, 1)

                    def q_high(i, b, c):
                        act.wait_ge(s_rp, i * 6 + (3 * c + 3))
                        for h in range(2):
                            last = nc.scalar.activation(qs[b][h][0:C, c * 512:(c + 1) * 512],
                                                        bank[2][h * C:(h + 1) * C, :], ACT.Copy)
                        last.then_inc(s_qh, 1)

                    def exps(j, u):
                        act.wait_ge(s_nm, j * 8 + (u + 1))
                        for h in range(2):
                            last = nc.scalar.activation(ex[u % 2][:, h, :], bank[4 + u % 2][:, h * S:(h + 1) * S],
                                                        ACT.Exp, bias=negm[:, u % 2, h:h + 1],
                                                        accum_out=den[:, u % 2, h:h + 1])
                        last.then_inc(s_ex, 1)

                    def probs_out(j, u):
                        act.wait_ge(s_tr, j * 8 + (u + 1))
                        r = u % 2
                        nc.scalar.activation(pT2[(u // 2) % 2][:, :, :, r * P:(r + 1) * P],
                                             bank[6][:].rearrange("p (h k n) -> p h k n", h=2, k=2),
                                             ACT.Copy).then_inc(s_ev, 1)

                    def values_high(j, b):
                        act.wait_ge(s_av, j * 4 + (b + 1))
                        nc.scalar.activation(c_h[b % 2][:], bank[7][:, 0:S], ACT.Copy).then_inc(s_ch, 1)

                    def slot(n, i, b, ii, do_s, do_q, loads):
                        j = i - 1
                        if do_s and n < NU:
                            exps(j, n)
                        if do_q and n == 4:
                            q_high(i, b, 0)
                        if do_s and 1 <= n <= NU:
                            probs_out(j, n - 1)
                        if do_q and n == 8:
                            q_high(i, b, 1)
                            if loads is not None:
                                m_high(i + 1)
                        if do_s and n >= 3 and n % 2:
                            values_high(j, (n - 3) // 2)
                        if do_q and n == 9 and loads is not None:
                            g_copy(i + 1)
                        if do_q and n == 10 and loads is not None:
                            if do_s:
                                act.wait_ge(s_y, i * 4)
                            f_high(i + 1, 1 - b)

                    def pre():
                        act.sem_inc(s_ev, 1)
                        norm_root(act, norm)
                        norm_act(act, norm)
                        act.wait_ge(s_kvT, 1)
                        for c in range(NCH):
                            last = nc.scalar.activation(ks_h[:, c * 512:(c + 1) * 512], bank[4 + c][:], ACT.Copy)
                        last.then_inc(s_ksh, 1)
                        m_high(0)
                        act.wait_ge(s_zero, 1)
                        g_copy(0)
                        f_high(0, 0)
                    run_pairs(act, slot, pre)

                @block.vector
                def _(dve):
                    seq = Seq(dve, "l1_att_vector_step")

                    def m_low(i):
                        dve.wait_ge(s_mh, i + 1)
                        for k in range(KD):
                            last = nc.vector.tensor_tensor(m_l[:, k, :], bank[k][:, 0:2 * CQ], m_h[:, k, :],
                                                           ALU.subtract)
                        last.then_inc(s_ml, 1)

                    def f_low(i, b):
                        dve.wait_ge(s_fh, i + 1)
                        nc.vector.tensor_tensor(f_l[b][:], bank[1][:, D:2 * D], f_h[b][:],
                                                ALU.subtract).then_inc(s_fl, 1)

                    def cos_sin(i, n):
                        dve.wait_ge(s_q, i * 6 + (n + 1))
                        q2 = bank[n % 2][:].rearrange("p (b s) -> p b s", b=2)
                        for dst, tab in ((qc, cosq), (qn, sinq)):
                            last = nc.vector.tensor_tensor(dst[n % 2][:].rearrange("p (b s) -> p b s", b=2), q2,
                                                           tab[:, n % JT:n % JT + 1, :].broadcast_to([P, 2, S]),
                                                           ALU.mult)
                        last.then_inc(s_cs, 1)

                    def q_low(i, b, c):
                        dve.wait_ge(s_qh, i * 2 + (c + 1))
                        for h in range(2):
                            cols = slice(c * 512, (c + 1) * 512)
                            last = nc.vector.tensor_tensor(qs[b][h][C:P, cols], bank[2][h * C:(h + 1) * C, :],
                                                           qs[b][h][0:C, cols], ALU.subtract)
                        last.then_inc(s_ql, 1)

                    def maxima(j, u):
                        dve.wait_ge(s_sc, j * 8 + (u + 1))
                        nc.vector.tensor_reduce(negm[:, u % 2, :], bank[4 + u % 2][:].rearrange(
                            "p (h n) -> p h n", h=2), AX_X, ALU.max, negate=True).then_inc(s_nm, 1)

                    def normalise(j, u):
                        dve.wait_ge(s_ex, j * 8 + (u + 1))
                        nc.vector.reciprocal(rden[:, u % 2, :], den[:, u % 2, :]).then_inc(s_rd, 1)
                        dve.wait_ge(s_rd, j * 8 + (u + 1))
                        for h in range(2):
                            last = nc.vector.tensor_scalar(pn[u % 2][:, h, :], ex[u % 2][:, h, :],
                                                           rden[:, u % 2, h:h + 1], None, ALU.mult)
                        last.then_inc(s_pn, 1)

                    def values_low(j, b):
                        dve.wait_ge(s_ch, j * 4 + (b + 1))
                        nc.vector.tensor_tensor(c_l[b % 2][:], bank[7][:, 0:S], c_h[b % 2][:],
                                                ALU.subtract).then_inc(s_cl, 1)

                    def add(j, b):
                        dve.wait_ge(s_y, j * 4 + (b + 1))
                        nc.vector.scalar_tensor_tensor(
                            out=x[:, 2 * b:2 * b + 2, :], in0=bank[3][:].rearrange("p (t d) -> p t d", t=2),
                            scalar=tg[:, 1:2], in1=x[:, 2 * b:2 * b + 2, :],
                            op0=ALU.mult, op1=ALU.add).then_inc(s_xa, 1)

                    def slot(n, i, b, ii, do_s, do_q, loads):
                        j = i - 1
                        if do_s and n < NU:
                            maxima(j, n)
                        if do_q and n in Q_AT:
                            cos_sin(i, Q_AT[n])
                        if do_s and n < NU:
                            normalise(j, n)
                        if do_q and n == 4:
                            q_low(i, b, 0)
                        if do_q and n == 8:
                            q_low(i, b, 1)
                            if loads is not None:
                                m_low(i + 1)
                        if do_s and n >= 3 and n % 2:
                            values_low(j, (n - 3) // 2)
                        if do_s and n >= 4 and n % 2 == 0:
                            add(j, (n - 4) // 2)
                        if do_q and n == 10 and loads is not None:
                            f_low(i + 1, 1 - b)

                    def pre():
                        dve.sem_inc(s_cl, 1)
                        dve.sem_inc(s_xa, 1)
                        dve.wait_ge(s_trigk, 16)
                        c4 = ctx_n[:].rearrange("p (b r) d -> p b r d", b=B)
                        k4 = kvc[:].rearrange("p (b r) d -> p b r d", b=B)
                        s4 = kvs[:].rearrange("p (b r) d -> p b r d", b=B)
                        hc = C // 2

                        def tab(which, lo, hi):
                            return trigk[:, which, :, lo:hi].unsqueeze(1).broadcast_to([P, B, 2, hi - lo])
                        seq.did(nc.vector.tensor_tensor(k4, c4, tab(0, 0, C), ALU.mult))
                        seq.did(nc.vector.tensor_tensor(s4[:, :, :, 0:hc], c4[:, :, :, hc:C], tab(1, 0, hc), ALU.mult))
                        seq.link(nc.vector.tensor_tensor(s4[:, :, :, hc:C], c4[:, :, :, 0:hc], tab(1, hc, C), ALU.mult))
                        for h in range(2):
                            last = nc.vector.tensor_tensor(kv[:, :, h * C:(h + 1) * C], kvc[:], kvs[:], ALU.add)
                        last.then_inc(s_kv, 1)
                        layer_norm(dve, seq, norm)
                        for g in range(NT // 2):
                            norm_dve_low(dve, norm, g)
                        dve.wait_ge(s_ksh, 1)
                        for c in range(NCH):
                            last = nc.vector.tensor_tensor(ks_l[:, c * 512:(c + 1) * 512], bank[4 + c][:],
                                                           ks_h[:, c * 512:(c + 1) * 512], ALU.subtract)
                        last.then_inc(s_ksl, 1)
                        m_low(0)
                        f_low(0, 0)
                        dve.wait_ge(s_trig, 32)
                    run_pairs(dve, slot, pre)
                    dve.wait_ge(s_xa, NPAIR * B + 1)

        def route1_act(act, s_logit, s_ract):
            act.wait_ge(s_logit, 1)
            nc.scalar.activation(sc[:], bank[7][:, 0:NT * E1].rearrange("p (t e) -> p t e", e=E1),
                                 ACT.Sigmoid).then_inc(s_ract, 1)

        def route1_dve(dve, seq, s_logit, s_ract, s_comb):
            dve.wait_ge(s_ract, 1)
            dve.wait_ge(s_bias, 16)
            seq.link(nc.vector.tensor_tensor(sel[:], sc[:], bias1[:].unsqueeze(1).broadcast_to([P, NT, E1]),
                                             ALU.add))
            pick_two(seq, sc, sel, E1)
            seq.link(nc.vector.tensor_reduce(rsum[:], oh[:], AX_X, ALU.add))
            seq.link(nc.vector.tensor_scalar(rsum[:], rsum[:], 1e-20, None, ALU.add))
            seq.link(nc.vector.reciprocal(rinv[:], rsum[:]))
            seq.link(nc.vector.tensor_scalar(rinv[:], rinv[:], tg[:, 3:4], None, ALU.mult))
            seq.did(nc.vector.tensor_tensor(comb[:, :, 0:E1], oh[:],
                                            rinv[:].unsqueeze(2).broadcast_to([P, NT, E1]), ALU.mult))
            seq.did(nc.vector.tensor_copy(comb[:, :, E1:N1], tg[:, 3:4].unsqueeze(1).broadcast_to([P, NT, 1])))
            dve.wait_ge(seq.sem, seq.n)

        ffn("l1_ffn", norms[3], N1, 14, a["w_ffn1"], 1, E1, route1_dve, False, E1, route1_act, None)

        with nc.Block() as block:
            @block.sync
            def _(sp):
                sp.dma_start(out, x[:]).then_inc(s_out, 16)
                sp.wait_ge(s_out, 16)


def rope_tables(length, dim):
    inv = (1.0 / 10000.0 ** (np.arange(0, dim, 2, dtype=np.float32) / np.float32(dim))).astype(np.float32)
    f = np.arange(length, dtype=np.float32)[:, None] * inv[None, :]
    return np.repeat(np.sin(f), 2, axis=-1).astype(np.float32), np.repeat(np.cos(f), 2, axis=-1).astype(np.float32)


def constants():
    sq, cq = rope_tables(S, CQ)
    half = CQ // 2
    turned = (np.arange(CQ) + half) % CQ
    sign = np.where(np.arange(CQ) < half, 1.0, -1.0).astype(np.float32)
    sq_m = (sq[:, turned] * sign[None, :]).T
    pack = lambda t: np.concatenate([t, t]).reshape(JT, P, S).transpose(1, 0, 2)
    sk, ck = rope_tables(S, C)
    sk = sk * np.where(np.arange(C) < C // 2, -1.0, 1.0).astype(np.float32)[None, :]
    trigk = np.stack([ck, sk]).reshape(2, 2, P, C).transpose(2, 0, 1, 3)
    sel0 = np.zeros((E0, P), np.float32)
    for e in range(E0):
        sel0[e, e * (P // E0):(e + 1) * (P // E0)] = 1.0
    return {
        "ident": np.eye(P, dtype=np.float32), "iota": np.arange(E1, dtype=np.float32), "sel0": sel0,
        "cosq": pack(cq.T), "sinq": pack(sq_m), "trigk": trigk,
    }


def layouts(v):
    g = {}
    tiles = lambda t: t.reshape(NT, P, -1).transpose(1, 0, 2)
    g["x"] = tiles(v["x"])
    g["ctx"] = tiles(v["ctx_512"])
    g["wqk"] = np.stack([v["L0_xattn_Wq"], v["L0_xattn_Wk"]], axis=1)
    g["gates"] = np.concatenate([v["g_xattn"], v["g_ffn"], v["L0_xattn_gamma_raw"].reshape(1)])
    r0 = np.zeros((D, E1), np.float32)
    r0[:, 0:E0] = v["L0_ffn_gate_weight"].T
    g["router"] = np.stack([r0, v["L1_ffn_gate_w"]]).reshape(2, KD, P, E1).transpose(2, 0, 1, 3)
    g["bias1"] = v["L1_ffn_expert_bias"]

    def ffn_tile(gate, up, down):
        return np.concatenate([gate[0:P], up[0:P], gate[P:D], up[P:D], down], axis=1)

    gu = v["L0_ffn_gate_up_weights"]
    gate = gu[:, 0:F0].reshape(P, R0, D)
    up = gu[:, F0:2 * F0].reshape(P, R0, D)
    down = v["L0_ffn_down_weights"].transpose(0, 2, 1).reshape(P, R0, D)
    w = [ffn_tile(gate[:, t].T, up[:, t].T, down[:, t]) for t in range(R0)]
    rows = (N0 - R0) * P
    sgu = np.zeros((2, rows, D), np.float32)
    sgu[:, 0:FS0] = v["L0_ffn_shared_gate_up"].reshape(2, FS0, D)
    sd = np.zeros((rows, D), np.float32)
    sd[0:FS0] = v["L0_ffn_shared_down"].T
    for t in range(N0 - R0):
        s = slice(t * P, (t + 1) * P)
        w.append(ffn_tile(sgu[0, s].T, sgu[1, s].T, sd[s]))
    g["w_ffn0"] = np.stack(w)
    gu1 = v["L1_ffn_experts_gate_up"]
    w = [ffn_tile(gu1[e, :, 0:F1], gu1[e, :, F1:], v["L1_ffn_experts_down"][e]) for e in range(E1)]
    w.append(ffn_tile(v["L1_ffn_shared_gate_w"], v["L1_ffn_shared_up_w"], v["L1_ffn_shared_down_w"]))
    g["w_ffn1"] = np.stack(w)

    wq = v["L1_xattn_Wq"].reshape(H, KH, D)
    wo = v["L1_xattn_Wo"].T.reshape(H, KH, D)
    turned = (np.arange(CQ) + CQ // 2) % CQ
    pw, pr = [], []
    for i in range(NPAIR):
        h0, h1 = 2 * i, 2 * i + 1
        pw.append(np.concatenate([wq[h0], wq[h1], v["L1_xattn_w_kc_q"][h0], v["L1_xattn_w_kc_q"][h1],
                                  v["L1_xattn_w_kc_kv"][h0], v["L1_xattn_w_kc_kv"][h1], wo[h0], wo[h1]], axis=1))
        qr = [v["L1_xattn_W_qr"][h].T for h in (h0, h1)]
        kr = [v["L1_xattn_W_kr"][h].T for h in (h0, h1)]
        pr.append(np.concatenate([qr[0], qr[1], qr[0][:, turned], qr[1][:, turned], kr[0], kr[1]], axis=1))
    g["pair_w"] = np.stack(pw)
    g["pair_r"] = np.stack(pr)
    return g


def kernel(**inputs):
    import concourse.bacc as bacc
    from concourse.bass_utils import run_bass_kernel_spmd

    arrays = {**layouts({k: np.asarray(v) for k, v in inputs.items()}), **constants()}
    arrays = {k: np.ascontiguousarray(v) for k, v in arrays.items()}
    nc = bacc.Bacc("TRN2", target_bir_lowering=False, num_devices=1)
    aps = {k: nc.dram_tensor(f"in_{k}", v.shape, F32, kind="ExternalInput").ap() for k, v in arrays.items()}
    out = nc.dram_tensor("out", (P, NT, D), F32, kind="ExternalOutput").ap()
    build(nc, aps, out)
    r = run_bass_kernel_spmd(nc, [{f"in_{k}": v for k, v in arrays.items()}], core_ids=[0])
    return r.results[0]["out"].transpose(1, 0, 2).reshape(B, S, D)
```

```python
from contextlib import ExitStack

import numpy as np

import concourse.bass as bass
from concourse import mybir

F32 = mybir.dt.float32
F32R = mybir.dt.float32r
U32 = mybir.dt.uint32
ALU = mybir.AluOpType
ACT = mybir.ActivationFunctionType
AX_X = mybir.AxisListType.X

P = 128
B, S, D = 4, 256, 256
T = B * S
NT = T // P
KD = D // P
NCH = T // 512
C = 64
TOPK = int(S * 0.3)
EPS = 1e-5
E0, F0, FS0 = 8, 176, 352
R0 = E0 * F0 // P
N0 = R0 + (FS0 + P - 1) // P
E1, F1 = 16, 128
N1 = E1 + 1
H, KH, CQ, R = 16, 128, 192, 64
NPAIR = H // 2
JT = 2 * CQ // P
WC = 2 * 2 * P + D
PW = 2 * D + 2 * CQ + 2 * C + 2 * D
PR = 2 * 2 * CQ + 2 * C
GOFF = KD * 2 * CQ
FOFF = GOFF + 2 * JT * P
FW = FOFF + D
NEG = -3.0e38


def build(nc, a, out):
    with ExitStack() as ctx:
        def sb(name, shape, dt=F32):
            return ctx.enter_context(nc.sbuf_tensor(name, shape, dt))

        def sem(name):
            return ctx.enter_context(nc.semaphore(name))

        def sems(prefix, *names):
            return [sem(f"{prefix}_{n}") for n in names]

        bank = [ctx.enter_context(nc.psum_tensor(f"bank{i}", [P, 512], F32)) for i in range(8)]

        x = sb("x", [P, NT, D])
        xn = sb("xn", [P, NT, D])
        xT_h = sb("xT_h", [P, KD, T], F32R)
        xT_l = sb("xT_l", [P, KD, T], F32R)
        ident = sb("ident", [P, P])
        iota = sb("iota", [P, E1])
        sel0 = sb("sel0", [E0, P])
        zero = sb("zero", [P, 512], F32R)
        gates = sb("gates", [P, 5])
        tg = sb("tg", [P, 5])
        cc = sb("cc", [P, 4])
        bn = sb("bn", [P, NT, 6])
        mv = sb("mv", [P, NT, 2])
        rstd = sb("rstd", [P, NT])
        var = sb("var", [P, NT])
        root = sb("root", [P, NT])
        ctx_n = sb("ctx_n", [P, NT, C])
        kv = sb("kv", [P, NT, 2 * C])
        ks_h = sb("ks_h", [P, T], F32R)
        ks_l = sb("ks_l", [P, T], F32R)
        w_raw = [sb(f"att_w_raw{i}", [P, FW]) for i in range(2)]
        rg_raw = sb("rg_raw", [P, 2, KD, E1])
        rg_h = sb("rg_h", [P, 2, KD, E1], F32R)
        rg_l = sb("rg_l", [P, 2, KD, E1], F32R)
        bias1 = sb("bias1", [P, E1])
        sc = sb("sc", [P, NT, E1])
        sel = sb("sel", [P, NT, E1])
        oh = sb("oh", [P, NT, E1])
        oh2 = sb("oh2", [P, NT, E1])
        rmax = sb("rmax", [P, NT])
        rsum = sb("rsum", [P, NT])
        rinv = sb("rinv", [P, NT])
        top8 = sb("top8", [P, NT, 8])
        idx8 = sb("idx8", [P, NT, 8], U32)
        idxf = sb("idxf", [P, NT, 2])
        comb = sb("comb", [P, NT, N1])
        combT = sb("combT", [E0, T])
        lgT = sb("lgT", [E1, 512])
        rows = sb("rows", [P, T])
        raw = [sb(f"ffn_raw{i}", [P, WC]) for i in range(2)]
        wt_h = [sb(f"ffn_w_h{i}", [P, WC], F32R) for i in range(2)]
        wt_l = [sb(f"ffn_w_l{i}", [P, WC], F32R) for i in range(2)]
        silu = [sb(f"silu{i}", [P, 512]) for i in range(2)]
        hid = [sb(f"hid{i}", [P, 512]) for i in range(2)]
        hid_h = [sb(f"hid_h{i}", [P, 512], F32R) for i in range(2)]
        hid_l = [sb(f"hid_l{i}", [P, 512], F32R) for i in range(2)]
        GU = 2 * 2 * P

        with ExitStack() as st:
            def lsb(name, shape, dt=F32):
                return st.enter_context(nc.sbuf_tensor(name, shape, dt))
            wqk = lsb("wqk", [C, 2, C])
            trigk = lsb("trigk", [P, 2, 2, C])
            kvc = lsb("kvc", [P, NT, C])
            kvs = lsb("kvs", [P, NT, C])
            ctxT = lsb("ctxT", [C, T])
            bmat = lsb("bmat", [C, C])
            pT = lsb("pT", [C, T])
            sim = lsb("sim", [P, NT, S])
            sig = lsb("sig", [P, NT, S])
            adj = lsb("adj", [P, NT, S])
            left = lsb("left", [P, NT, S])
            best = lsb("best", [P, NT, 8])
            kept = lsb("kept", [P, NT // 2])
            pw = [lsb(f"pair_w{i}", [P, PW]) for i in range(2)]
            pr = [lsb(f"pair_r{i}", [R, PR]) for i in range(2)]
        with ExitStack() as st:
            def lsb(name, shape, dt=F32):
                return st.enter_context(nc.sbuf_tensor(name, shape, dt))
            cosq = lsb("cosq", [P, JT, S])
            sinq = lsb("sinq", [P, JT, S])
            w_h = [lsb(f"att_w_h{i}", [P, FOFF], F32R) for i in range(2)]
            w_l = [lsb(f"att_w_l{i}", [P, FOFF], F32R) for i in range(2)]
            f_h = [lsb(f"att_f_h{i}", [P, D], F32R) for i in range(2)]
            f_l = [lsb(f"att_f_l{i}", [P, D], F32R) for i in range(2)]
            qr = [lsb(f"qr{i}", [P, 2, 512]) for i in range(2)]
            qr_h = [lsb(f"qr_h{i}", [P, 2, 512], F32R) for i in range(2)]
            qr_l = [lsb(f"qr_l{i}", [P, 2, 512], F32R) for i in range(2)]
            qs = [[lsb(f"qs{i}_{h}", [P, T], F32R) for h in range(2)] for i in range(2)]
            negm = lsb("negm", [P, 2, 2])
            den = lsb("den", [P, 2, 2])
            rden = lsb("rden", [P, 2, 2])
            ex = [lsb(f"ex{i}", [P, 2, S]) for i in range(2)]
            pn = [lsb(f"pn{i}", [P, 2, S]) for i in range(2)]
            pT2 = [lsb(f"probsT{i}", [P, 2, 2, S]) for i in range(2)]
            c_h = [lsb(f"c_h{i}", [P, S], F32R) for i in range(2)]
            c_l = [lsb(f"c_l{i}", [P, S], F32R) for i in range(2)]
        folds = nc.dram_tensor("folds", (NPAIR, P, FW), F32, kind="Internal").ap()

        class Seq:
            def __init__(self, eng, name):
                self.eng, self.sem, self.n = eng, sem(name), 0

            def did(self, ins):
                self.n += 1
                ins.then_inc(self.sem, 1)

            def wait(self):
                self.eng.wait_ge(self.sem, self.n)

            def link(self, ins):
                self.did(ins)
                self.wait()

        s_ctx, s_wqk, s_x, s_const, s_rg, s_bias, s_trigk, s_trig = sems(
            "loaded", "ctx", "wqk", "x", "constants", "router", "bias", "rope_k", "rope_q")
        s_gates = sem("gates_loaded")
        s_out = sem("out_stored")
        s_zr = sem("zero_rounded")
        s_xs = sem("l0_att_norm_scaled")
        s_gact, s_rgh, s_rgl, s_zz = sem("gates_activated"), sem("router_h_ready"), sem("router_l_ready"), sem("zero_ready")
        s_kv, s_kvT, s_ksh, s_ksl = sems("kv", "roped", "transposed", "h_ready", "l_ready")
        s_ct, s_ctc, s_bm, s_bmc, s_pt, s_ptc, s_sim, s_simc, s_sig, s_adj, s_adjT, s_x1, s_upd = sems(
            "l0_att", "ctx_transposed", "ctxT_ready", "bmat_done", "bmat_ready", "pT_done", "pT_ready", "sim_done",
            "sim_ready", "sigmoid_ready", "adj_ready", "adj_transposed", "x_plus_norm_ready", "updated")
        s_left = sem("l0_att_left_ready")
        s_pw = [sem(f"pair_w{i}_loaded") for i in range(2)]
        s_stored = [sem(f"folds{i}_stored") for i in range(2)]
        s_zero, s_f, s_fcp = sems("folds", "zeroed", "done", "parts_copied")
        s_w = [sem(f"att_w{i}_loaded") for i in range(2)]
        s_wh, s_wl, s_fh, s_fl = sems("att", "w_h_ready", "w_l_ready", "f_h_ready", "f_l_ready")
        s_q, s_cs, s_crh, s_crl, s_rp, s_qh, s_ql = sems(
            "q", "done", "cos_sin_ready", "cos_sin_h_ready", "cos_sin_l_ready", "rope_done", "stack_h_ready",
            "stack_l_ready")
        s_sc, s_nm, s_ex, s_rd, s_pn, s_tr, s_ev = sems(
            "softmax", "scores_done", "max_ready", "exp_ready", "inverse_sum_ready", "probs_ready",
            "probs_transposed", "probsT_ready")
        s_av, s_ch, s_cl, s_y, s_xa = sems(
            "values", "done", "h_ready", "l_ready", "projected", "added")

        class Norm:
            def __init__(self, sems_of, i, hf, banks):
                self.i, self.hf, self.banks = i, hf, banks
                self.var, self.root, self.ln, self.tr, self.h, self.l = sems_of
                self.tiles = slice(4 * hf, 4 * hf + 4)

            def stats(self, seq):
                seq.wait()
                for t in range(4 * self.hf, 4 * self.hf + 4):
                    seq.did(nc.vector.bn_stats(bn[:, t, :], x[:, t, :]))
                seq.wait()
                for t in range(4 * self.hf, 4 * self.hf + 4):
                    seq.did(nc.vector.bn_aggr(mv[:, t, :], bn[:, t, :]))
                seq.wait()
                nc.vector.tensor_scalar(var[:, self.tiles], mv[:, self.tiles, 1], EPS, None,
                                        ALU.add).then_inc(self.var, 1)

            def act_root(self, act):
                act.wait_ge(self.var, self.i + 1)
                nc.scalar.activation(root[:, self.tiles], var[:, self.tiles], ACT.Sqrt).then_inc(self.root, 1)

            def scale(self, dve, seq):
                r, w, v = rstd[:, self.tiles], root[:, self.tiles], var[:, self.tiles]
                dve.wait_ge(self.root, self.i + 1)
                seq.link(nc.vector.reciprocal(r, w))
                seq.link(nc.vector.tensor_tensor(w, r, r, ALU.mult))
                seq.link(nc.vector.tensor_tensor(w, w, v, ALU.mult))
                seq.link(nc.vector.tensor_scalar(w, w, -0.5, 1.5, ALU.mult, ALU.add))
                seq.link(nc.vector.tensor_tensor(r, r, w, ALU.mult))
                for t in range(4 * self.hf, 4 * self.hf + 4):
                    ins = nc.vector.tensor_scalar(xn[:, t, :], x[:, t, :], mv[:, t, 0:1], rstd[:, t:t + 1],
                                                  ALU.subtract, ALU.mult)
                    if t % 2:
                        ins.then_inc(self.ln, 1)

            def views(self, g):
                t0 = 4 * self.hf + 2 * g
                cols = slice(t0 * P, (t0 + 2) * P)
                return bank[self.banks[g]][:].rearrange("p (k n) -> p k n", k=KD), xT_h[:, :, cols], xT_l[:, :, cols]

            def pe_transpose(self, pe):
                for g in range(2):
                    pe.wait_ge(self.ln, 2 * self.i + g + 1)
                    for k in range(KD):
                        for j in range(2):
                            last = nc.tensor.matmul(
                                bank[self.banks[g]][:, k * 256 + j * P:k * 256 + (j + 1) * P],
                                xn[:, 4 * self.hf + 2 * g + j, k * P:(k + 1) * P], ident[:],
                                start=True, stop=True, is_transpose=True)
                    last.then_inc(self.tr, 1)

            def act_high(self, act):
                for g in range(2):
                    b, h, _ = self.views(g)
                    act.wait_ge(self.tr, 2 * self.i + g + 1)
                    nc.scalar.activation(h, b, ACT.Copy).then_inc(self.h, 1)

            def low(self, dve):
                for g in range(2):
                    b, h, lo = self.views(g)
                    dve.wait_ge(self.h, 2 * self.i + g + 1)
                    nc.vector.tensor_tensor(lo, b, h, ALU.subtract).then_inc(self.l, 1)

            def pe_whole(self, pe):
                pe.wait_ge(self.l, 2 * self.i + 2)

        norm_steps = ("variance_ready", "root_ready", "normed", "transposed", "xT_h_ready", "xT_l_ready")
        first_norm, later_norm = sems("l0_att_norm", *norm_steps[0:3]) + [None] * 3, sems("norm", *norm_steps)
        n_l0att = [Norm(first_norm, hf, hf, None) for hf in range(2)]
        n_ffn0 = [Norm(later_norm, hf, hf, ((5, 6), (6, 7))[hf]) for hf in range(2)]
        n_att = [Norm(later_norm, 2 + hf, hf, (6, 7)) for hf in range(2)]
        n_ffn1 = [Norm(later_norm, 4 + hf, hf, (0, 1) if hf == 0 else (6, 7)) for hf in range(2)]

        route_sems = [sems("l0_route", "logitsT_done", "logitsT_ready", "logits_done", "activated", "shifted", "comb_ready", "comb_transposed",
                           "combT_ready", "rows_done", "rows_ready"),
                      sems("l1_route", "logitsT_done", "logitsT_ready", "logits_done", "activated") + [None] * 6]

        class Router:
            def __init__(self, layer, hf, norm, tbank, lbank, cbank=None):
                self.layer, self.hf, self.norm, self.tbank, self.lbank, self.cbank = layer, hf, norm, tbank, lbank, cbank
                self.ne = (E0, E1)[layer]
                self.lT, self.lTc, self.logit, self.act, self.shift, self.comb, self.cT, self.cTc, self.row, self.rowc = route_sems[layer]
                self.ts = slice(4 * hf, 4 * hf + 4)
                self.lg = bank[lbank][:, 0:4 * self.ne].rearrange("p (t e) -> p t e", e=self.ne)

            def pe_logits(self, pe):
                self.norm.pe_whole(pe)
                pe.wait_ge(s_rgl, 1)
                ne, cols = self.ne, slice(self.hf * 512, (self.hf + 1) * 512)
                parts = [(xh, rh, k) for xh, rh in ((xT_h, rg_h), (xT_h, rg_l), (xT_l, rg_h)) for k in range(KD)]
                for m, (xh, rh, k) in enumerate(parts):
                    last = nc.tensor.matmul(bank[self.tbank][0:ne, :], rh[:, self.layer, k, 0:ne], xh[:, k, cols],
                                            start=(m == 0), stop=(m == len(parts) - 1))
                last.then_inc(self.lT, 1)

            def act_logits(self, act):
                act.wait_ge(self.lT, self.hf + 1)
                nc.scalar.activation(lgT[0:self.ne, :], bank[self.tbank][0:self.ne, :],
                                     ACT.Copy).then_inc(self.lTc, 1)

            def pe_turn_logits(self, pe):
                pe.wait_ge(self.lTc, self.hf + 1)
                ne = self.ne
                for t in range(4):
                    last = nc.tensor.matmul(bank[self.lbank][:, t * ne:(t + 1) * ne], lgT[0:ne, t * P:(t + 1) * P],
                                            ident[0:ne, 0:ne], start=True, stop=True, is_transpose=True)
                last.then_inc(self.logit, 1)

            def pick_two(self, seq, choose):
                ne, ts = self.ne, self.ts
                for t in range(4 * self.hf, 4 * self.hf + 4):
                    seq.did(nc.vector.max(top8[:, t, :], choose[:, t, 0:ne]))
                seq.wait()
                for t in range(4 * self.hf, 4 * self.hf + 4):
                    seq.did(nc.vector.max_index(idx8[:, t, :], top8[:, t, :], choose[:, t, 0:ne]))
                seq.wait()
                seq.link(nc.vector.tensor_copy(idxf[:, ts, :], idx8[:, ts, 0:2]))
                io = iota[:, 0:ne].unsqueeze(1).broadcast_to([P, 4, ne])
                for o, j in ((oh, 0), (oh2, 1)):
                    seq.did(nc.vector.tensor_tensor(o[:, ts, 0:ne], io,
                                                    idxf[:, ts, j:j + 1].broadcast_to([P, 4, ne]), ALU.is_equal))
                seq.wait()
                seq.link(nc.vector.tensor_tensor(oh[:, ts, 0:ne], oh[:, ts, 0:ne], oh2[:, ts, 0:ne], ALU.add))
                seq.link(nc.vector.tensor_tensor(oh[:, ts, 0:ne], oh[:, ts, 0:ne], sc[:, ts, 0:ne], ALU.mult))

        def wide(col, ne):
            return col.unsqueeze(2).broadcast_to([P, 4, ne])

        def route0(r, dve, seq):
            ts = r.ts
            dve.wait_ge(r.logit, r.hf + 1)
            seq.link(nc.vector.tensor_reduce(rmax[:, ts], r.lg, AX_X, ALU.max))
            nc.vector.tensor_tensor(sel[:, ts, 0:E0], r.lg, wide(rmax[:, ts], E0), ALU.subtract).then_inc(r.shift, 1)
            dve.wait_ge(r.act, r.hf + 1)
            seq.link(nc.vector.tensor_reduce(rsum[:, ts], sc[:, ts, 0:E0], AX_X, ALU.add))
            seq.link(nc.vector.reciprocal(rinv[:, ts], rsum[:, ts]))
            seq.link(nc.vector.tensor_tensor(sc[:, ts, 0:E0], sc[:, ts, 0:E0], wide(rinv[:, ts], E0), ALU.mult))
            r.pick_two(seq, sc)
            nc.vector.tensor_scalar(comb[:, ts, 0:E0], oh[:, ts, 0:E0], tg[:, 2:3], None,
                                    ALU.mult).then_inc(r.comb, 1)

        def route0_act(r, act):
            act.wait_ge(r.shift, r.hf + 1)
            nc.scalar.activation(sc[:, r.ts, 0:E0], sel[:, r.ts, 0:E0], ACT.Exp).then_inc(r.act, 1)

        def rows_pe(r, pe):
            pe.wait_ge(r.comb, r.hf + 1)
            for j in range(4):
                last = nc.tensor.matmul(bank[r.cbank][0:E0, j * P:(j + 1) * P], comb[:, 4 * r.hf + j, 0:E0], ident[:],
                                        start=True, stop=True, is_transpose=True)
            last.then_inc(r.cT, 1)
            pe.wait_ge(r.cTc, r.hf + 1)
            nc.tensor.matmul(bank[6][:], sel0[:], combT[:, r.hf * 512:(r.hf + 1) * 512],
                             start=True, stop=True).then_inc(r.row, 1)

        def rows_act(r, act):
            act.wait_ge(r.cT, r.hf + 1)
            nc.scalar.activation(combT[:, r.hf * 512:(r.hf + 1) * 512], bank[r.cbank][0:E0, :],
                                 ACT.Copy).then_inc(r.cTc, 1)
            act.wait_ge(r.row, r.hf + 1)
            nc.scalar.activation(rows[:, r.hf * 512:(r.hf + 1) * 512], bank[6][:], ACT.Copy).then_inc(r.rowc, 1)

        def route1_act(r, act):
            act.wait_ge(r.logit, r.hf + 1)
            nc.scalar.activation(sc[:, r.ts, :], r.lg, ACT.Sigmoid).then_inc(r.act, 1)

        def route1(r, dve, seq):
            ts = r.ts
            dve.wait_ge(r.act, r.hf + 1)
            dve.wait_ge(s_bias, 16)
            seq.link(nc.vector.tensor_tensor(sel[:, ts, :], sc[:, ts, :],
                                             bias1[:].unsqueeze(1).broadcast_to([P, 4, E1]), ALU.add))
            r.pick_two(seq, sel)
            seq.link(nc.vector.tensor_reduce(rsum[:, ts], oh[:, ts, :], AX_X, ALU.add))
            seq.link(nc.vector.tensor_scalar(rsum[:, ts], rsum[:, ts], 1e-20, None, ALU.add))
            seq.link(nc.vector.reciprocal(rinv[:, ts], rsum[:, ts]))
            seq.link(nc.vector.tensor_scalar(rinv[:, ts], rinv[:, ts], tg[:, 3:4], None, ALU.mult))
            seq.did(nc.vector.tensor_tensor(comb[:, ts, 0:E1], oh[:, ts, :], wide(rinv[:, ts], E1), ALU.mult))
            seq.did(nc.vector.tensor_copy(comb[:, ts, E1:N1], tg[:, 3:4].unsqueeze(1).broadcast_to([P, 4, 1])))
            seq.wait()

        route = [[Router(0, 0, n_ffn0[0], 5, 6, 5), Router(0, 1, n_ffn0[1], 7, 6, 7)],
                 [Router(1, 0, n_ffn1[0], 1, 2), Router(1, 1, n_ffn1[1], 7, 6)]]

        class Ffn:
            def __init__(self, layer, n, loops):
                self.layer, self.n, self.loops = layer, n, loops
                self.weights = a[f"w_ffn{layer}"]
                self.raw_g = [sem(f"l{layer}_ffn_raw_gateup{i}_loaded") for i in range(2)]
                self.raw_d = [sem(f"l{layer}_ffn_raw_down{i}_loaded") for i in range(2)]
                (self.wgh, self.wgl, self.wdh, self.wdl, self.gu, self.silu, self.prod, self.hid, self.hh, self.hl,
                 self.down, self.acc) = sems(
                    f"l{layer}_ffn", "gateup_h_ready", "gateup_l_ready", "down_h_ready", "down_l_ready",
                    "gateup_done", "silu_ready", "product_ready", "hidden_ready", "hidden_h_ready",
                    "hidden_l_ready", "down_done", "added")

            def run(self, eng, body, hooks):
                for c in range(2 * self.n - 1):
                    first, count = self.loops[c // self.n]
                    at = c % self.n - first
                    if at <= 0 or at >= count:
                        if c in hooks:
                            hooks[c]()
                    if at == 0:
                        with eng.Fori(0, count // 2) as ii:
                            for j in range(2):
                                body(Step(self.n, c + j, ii))
                    elif at < 0 or at >= count:
                        body(Step(self.n, c))

            def load_gateup(self, sp, st):
                sp.dma_start(raw[st.b][:, 0:GU], self.weights[st.e][:, 0:GU]).then_inc(self.raw_g[st.b], 16)

            def load_down(self, sp, st):
                sp.dma_start(raw[st.b][:, GU:WC], self.weights[st.e][:, GU:WC]).then_inc(self.raw_d[st.b], 16)

            def first_loads(self, sp):
                for c in range(2):
                    self.load_gateup(sp, Step(self.n, c))
                    self.load_down(sp, Step(self.n, c))

            def low_gateup(self, pool, st):
                b = st.b
                pool.wait_ge(self.wgh, st.k + 1)
                nc.gpsimd.tensor_tensor(wt_l[b][:, 0:GU], raw[b][:, 0:GU], wt_h[b][:, 0:GU],
                                        ALU.subtract).then_inc(self.wgl, 1)

            def low_down(self, pool, st):
                b = st.b
                pool.wait_ge(self.wdh, st.k + 1)
                nc.gpsimd.tensor_tensor(wt_l[b][:, GU:WC], raw[b][:, GU:WC], wt_h[b][:, GU:WC],
                                        ALU.subtract).then_inc(self.wdl, 1)

            def split_gateup(self, act, st):
                act.wait_ge(self.raw_g[st.b], st.loads * 16)
                nc.scalar.activation(wt_h[st.b][:, 0:GU], raw[st.b][:, 0:GU], ACT.Copy).then_inc(self.wgh, 1)

            def split_down(self, act, st):
                act.wait_ge(self.raw_d[st.b], st.loads * 16)
                nc.scalar.activation(wt_h[st.b][:, GU:WC], raw[st.b][:, GU:WC], ACT.Copy).then_inc(self.wdh, 1)

            def act_silu(self, act, st):
                act.wait_ge(self.gu, st.k + 1)
                nc.scalar.activation(silu[st.b][:], bank[2 * st.b][:], ACT.Silu).then_inc(self.silu, 1)

            def act_high(self, act, st):
                act.wait_ge(self.hid, st.k + 1)
                nc.scalar.activation(hid_h[st.b][:], hid[st.b][:], ACT.Copy).then_inc(self.hh, 1)

            def hidden(self, dve, st):
                b = st.b
                dve.wait_ge(self.silu, st.k + 1)
                up = bank[2 * b + 1]
                if self.layer == 1:
                    nc.vector.tensor_tensor(hid[b][:], silu[b][:], up[:], ALU.mult).then_inc(self.hid, 1)
                elif not st.loop and st.e >= R0:
                    nc.vector.scalar_tensor_tensor(out=hid[b][:], in0=silu[b][:], scalar=tg[:, 2:3], in1=up[:],
                                                   op0=ALU.mult, op1=ALU.mult).then_inc(self.hid, 1)
                else:
                    nc.vector.tensor_tensor(silu[b][:], silu[b][:], up[:], ALU.mult).then_inc(self.prod, 1)
                    dve.wait_ge(self.prod, st.k + (1 - (N0 - R0) * st.hf))
                    nc.vector.tensor_tensor(hid[b][:], silu[b][:], rows[:, st.hf * 512:(st.hf + 1) * 512],
                                            ALU.mult).then_inc(self.hid, 1)

            def low_on_pool(self, st):
                return self.layer == 0 and st.c < rounds

            def low(self, eng, vec, st):
                eng.wait_ge(self.hh, st.k + 1)
                vec.tensor_tensor(hid_l[st.b][:], hid[st.b][:], hid_h[st.b][:],
                                        ALU.subtract).then_inc(self.hl, 1)

            def add(self, dve, st):
                dve.wait_ge(self.down, st.k + 1)
                for t in range(4):
                    row = comb[:, 4 * st.hf + t, :]
                    col = row[:, bass.ds(st.e, 1)] if st.loop else row[:, st.e:st.e + 1]
                    last = nc.vector.scalar_tensor_tensor(
                        out=x[:, 4 * st.hf + t, :], in0=bank[4 + t // 2][:, (t % 2) * D:(t % 2 + 1) * D],
                        scalar=col, in1=x[:, 4 * st.hf + t, :], op0=ALU.mult, op1=ALU.add)
                last.then_inc(self.acc, 1)

            def add_sum(self, dve, hf):
                dve.wait_ge(self.down, self.n * (hf + 1))
                for j in range(2):
                    t = 4 * hf + 2 * j
                    last = nc.vector.tensor_tensor(x[:, t:t + 2, :], bank[4 + j][:].rearrange("p (t d) -> p t d", t=2),
                                                   x[:, t:t + 2, :], ALU.add)
                last.then_inc(self.acc, 1)

            def gateup(self, pe, st):
                pe.wait_ge(self.wgl, st.k + 1)
                for g in range(2):
                    m = 0
                    for wp, xp in ((wt_h, xT_h), (wt_h, xT_l), (wt_l, xT_h)):
                        for kt in range(KD):
                            last = nc.tensor.matmul(
                                bank[2 * st.b + g][:], wp[st.b][:, (2 * kt + g) * P:(2 * kt + g + 1) * P],
                                xp[:, kt, st.hf * 512:(st.hf + 1) * 512], start=(m == 0), stop=(m == 5))
                            m += 1
                last.then_inc(self.gu, 1)

            def clear_sum(self, pe, hf):
                if hf:
                    pe.wait_ge(self.acc, hf)
                for j in range(2):
                    nc.tensor.matmul(bank[4 + j][:], zero[:, 0:P], zero[:], start=True, stop=False,
                                     skip_group_check=True)

            def pe_down(self, pe, st):
                pe.wait_ge(self.hl, st.k + 1)
                pe.wait_ge(self.wdl, st.k + 1)
                if self.layer == 1 and (st.loop or st.k):
                    pe.wait_ge(self.acc, st.k)
                for t in range(4):
                    for m, (hp, wp) in enumerate(((hid_h, wt_h), (hid_h, wt_l), (hid_l, wt_h))):
                        last = nc.tensor.matmul(bank[4 + t // 2][:, (t % 2) * D:(t % 2 + 1) * D],
                                                hp[st.b][:, t * P:(t + 1) * P], wp[st.b][:, GU:WC],
                                                start=(self.layer == 1 and m == 0), stop=(m == 2),
                                                skip_group_check=(self.layer == 0))
                last.then_inc(self.down, 1)

            def prog_sp(self, sp, hooks):
                for c in range(2):
                    sp.wait_ge(self.wgl, c + 1)
                    self.load_gateup(sp, Step(self.n, c + 2))
                sp.wait_ge(self.wdl, 1)
                self.load_down(sp, Step(self.n, 2))

                def body(st):
                    if st.loop or st.k + 4 < 2 * self.n:
                        sp.wait_ge(self.wgl, st.k + 3)
                        self.load_gateup(sp, st.plus(4))
                    if st.loop or st.k + 3 < 2 * self.n:
                        sp.wait_ge(self.wdl, st.k + 2)
                        self.load_down(sp, st.plus(3))
                self.run(sp, body, hooks)

            def prog_pool(self, pool, hooks):
                def body(st):
                    if st.loop or st.k + 2 < 2 * self.n:
                        self.low_gateup(pool, st.plus(2))
                    self.low_down(pool, st.plus(1))
                    if self.low_on_pool(st):
                        self.low(pool, nc.gpsimd, st.plus(1))
                self.run(pool, body, hooks)

            def first_lows(self, pool):
                self.low_gateup(pool, Step(self.n, 0))
                self.low_down(pool, Step(self.n, 0))
                self.low_gateup(pool, Step(self.n, 1))

            def prog_act(self, act, hooks, mid):
                def body(st):
                    nx = st.plus(1)
                    if st.loop or st.k + 2 < 2 * self.n:
                        self.split_gateup(act, st.plus(2))
                    self.act_silu(act, nx)
                    if st.loop or st.k:
                        act.wait_ge(self.down, st.k)
                    self.split_down(act, nx)
                    if not st.loop and st.k in mid:
                        mid[st.k]()
                    self.act_high(act, nx)
                self.run(act, body, hooks)

            def first_splits(self, act):
                self.split_gateup(act, Step(self.n, 0))
                self.split_down(act, Step(self.n, 0))
                self.split_gateup(act, Step(self.n, 1))

            def prog_pe(self, pe, hooks):
                def body(st):
                    self.gateup(pe, st.plus(1))
                    if self.layer == 0 and not st.loop and st.e == 0:
                        self.clear_sum(pe, st.hf)
                    self.pe_down(pe, st)
                self.run(pe, body, hooks)
                self.pe_down(pe, Step(self.n, 2 * self.n - 1))

            def prog_dve(self, dve, hooks, beside):
                def body(st):
                    nx = st.plus(1)
                    beside(st, 0)
                    self.hidden(dve, nx)
                    beside(st, 1)
                    if self.layer == 1:
                        self.add(dve, st)
                    elif not st.loop and st.k == self.n:
                        self.add_sum(dve, 0)
                    if not self.low_on_pool(st):
                        if self.layer == 0 and st.c == rounds:
                            dve.wait_ge(self.hl, st.k + 1)
                        self.low(dve, nc.vector, nx)
                self.run(dve, body, hooks)
                if self.layer == 1:
                    self.add(dve, Step(self.n, 2 * self.n - 1))
                else:
                    self.add_sum(dve, 1)

        class Step:
            def __init__(self, n, c, ii=None):
                self.n, self.c, self.ii = n, c, ii
                self.loop = ii is not None
                self.hf, self.b = c // n, c % 2
                if self.loop:
                    self.k, self.e, self.loads = ii * 2 + c, ii * 2 + c % n, ii + (c // 2 + 1)
                else:
                    self.k, self.e, self.loads = c, c % n, c // 2 + 1

            def plus(self, d):
                return Step(self.n, self.c + d, self.ii)

        ffn0 = Ffn(0, N0, ((1, 8), (3, 6)))
        ffn1 = Ffn(1, N1, ((1, 12), (1, 12)))
        ffn0_first, ffn1_first = Step(N0, 0), Step(N1, 0)
        s_top, s_rep, s_kept = sems("topk", "eight_found", "eight_taken", "least_kept")
        kth, rounds = (TOPK - 1) % 8, (TOPK + 7) // 8
        HN = NT // 2

        def wq_of(b, h, k):
            return pw[b][:, h * D + k * P:h * D + (k + 1) * P]

        def wkq_of(b, h):
            return pw[b][:, 2 * D + h * CQ:2 * D + (h + 1) * CQ]

        def wkv_of(b, h):
            o = 2 * D + 2 * CQ + h * C
            return pw[b][:, o:o + C]

        def wo_of(b, h):
            o = 2 * D + 2 * CQ + 2 * C + h * D
            return pw[b][:, o:o + D]

        def m_of(w, k, j):
            return w[:, k * 2 * CQ + j * P:k * 2 * CQ + (j + 1) * P]

        def g_of(w, j):
            return w[:, GOFF + j * P:GOFF + (j + 1) * P]

        Q_AT = {0: 1, 2: 2, 4: 3, 6: 4, 8: 5}
        EARLY = 11
        R_AT = {1: 0, 3: 1, 5: 2, 7: 3, 9: 4, 10: 5}
        QH_AT = {5: 0, 10: 1}

        Q3_AT = {m: n for n, m in Q_AT.items()}[JT]

        def q_here(n, i, do_q):
            return do_q and n in Q_AT and not (isinstance(i, int) and i == 0 and Q_AT[n] == 1)

        def early(n, i, do_q):
            return do_q and n == EARLY and not (isinstance(i, int) and i == NPAIR - 1)
        F_AT, W_AT = 1, {2: 0, 5: 1, 9: 2}
        WPARTS, WSTEP = 3, FOFF // 3
        LAG = 2
        SLOTS = 10 + LAG
        VALUES_AT = {2 * b + 2 + LAG: b for b in range(B)}
        PROJECT_AT = {2 * b + 3 + LAG: b for b in range(B)}
        NU = NT

        def run_pairs(slot, eng, first, tail):
            for n in range(SLOTS):
                if n in first:
                    first[n]()
                slot(n, 0, 0, 1, False, True)
            with eng.Fori(0, (NPAIR - 2) // 2) as ii:
                for h in range(2):
                    for n in range(SLOTS):
                        slot(n, ii * 2 + (1 + h), (1 + h) % 2, ii + (1 + h), True, True)
            for n in range(SLOTS):
                slot(n, NPAIR - 1, (NPAIR - 1) % 2, NPAIR // 2, True, True)
            for n in range(SLOTS):
                if n in tail:
                    tail[n]()
                slot(n, NPAIR, NPAIR % 2, NPAIR // 2 + 1, True, False)

        with nc.Block() as block:
            @block.sync
            def _(sp):
                sp.dma_start(ctx_n[:], a["ctx"]).then_inc(s_ctx, 16)
                sp.dma_start(wqk[:], a["wqk"]).then_inc(s_wqk, 16)
                sp.dma_start(ident[:], a["ident"]).then_inc(s_const, 16)
                sp.dma_start(trigk[:], a["trigk"]).then_inc(s_trigk, 16)
                sp.dma_start(x[:], a["x"]).then_inc(s_x, 16)

                def load_pair(i):
                    pair = (i + 2) % NPAIR
                    sp.dma_start(pw[i % 2][:], a["pair_w"][pair]).then_inc(s_pw[i % 2], 16)
                    sp.dma_start(pr[i % 2][:], a["pair_r"][pair]).then_inc(s_pw[i % 2], 16)

                load_pair(0)
                load_pair(1)
                sp.dma_start(gates[:], a["gates"].partition_broadcast(P)).then_inc(s_gates, 16)
                sp.dma_start(iota[:], a["iota"].partition_broadcast(P)).then_inc(s_gates, 16)
                sp.dma_start(sel0[:], a["sel0"]).then_inc(s_gates, 16)
                sp.dma_start(rg_raw[:], a["router"]).then_inc(s_rg, 16)
                sp.dma_start(bias1[:], a["bias1"].partition_broadcast(P)).then_inc(s_bias, 16)
                ffn0.first_loads(sp)
                for i in range(NPAIR - 2):
                    sp.wait_ge(s_f, 3 * (i + 1))
                    load_pair(i + 2)
                    sp.wait_ge(s_fcp, 7 * (i + 1))
                    sp.dma_start(folds[i + 2], w_raw[i % 2][:]).then_inc(s_stored[i % 2], 16)

                def load_folds(i, b):
                    sp.dma_start(w_raw[b][:], folds[i]).then_inc(s_w[b], 16)

                def load_attention():
                    sp.wait_ge(s_upd, B)
                    for b in range(2):
                        sp.wait_ge(s_stored[b], 16 * (NPAIR // 2 - 1))
                    sp.dma_start(cosq[:], a["cosq"]).then_inc(s_trig, 16)
                    sp.dma_start(sinq[:], a["sinq"]).then_inc(s_trig, 16)

                ffn0.prog_sp(sp, {N0: load_attention})
                sp.wait_ge(ffn0.wdl, 2 * N0)
                ffn1.first_loads(sp)
                with sp.Fori(0, (NPAIR - 2) // 2) as ii:
                    for b in range(2):
                        sp.wait_ge(s_wl, ii * (2 * WPARTS) + WPARTS * (b + 1))
                        sp.wait_ge(s_fl, ii * 2 + (b + 1))
                        load_folds(ii * 2 + (b + 2), b)

                def store_first_half():
                    sp.wait_ge(ffn1.acc, N1)
                    sp.dma_start(out[:, 0:HN, :], x[:, 0:HN, :]).then_inc(s_out, 16)
                ffn1.prog_sp(sp, {2 * N1 - 3: store_first_half})
                sp.wait_ge(ffn1.acc, 2 * N1)
                sp.dma_start(out[:, HN:NT, :], x[:, HN:NT, :]).then_inc(s_out, 16)
                sp.wait_ge(s_out, 32)

            @block.gpsimd
            def _(pool):
                for i in range(2):
                    nc.gpsimd.memset(w_raw[i][:, GOFF:FOFF], 0.0).then_inc(s_zero, 1)
                nc.gpsimd.memset(hid[0][:], 0.0).then_inc(s_zz, 1)

                def add_norm(hf):
                    for g in range(2):
                        pool.wait_ge(n_l0att[hf].ln, 2 * hf + g + 1)
                        ts = slice(HN * hf + 2 * g, HN * hf + 2 * g + 2)
                        nc.gpsimd.tensor_scalar(xn[:, ts, :], xn[:, ts, :], cc[:, 1:2], None,
                                                ALU.mult).then_inc(s_xs, 1)
                        pool.wait_ge(s_xs, 2 * hf + g + 1)
                        nc.gpsimd.tensor_tensor(x[:, ts, :], x[:, ts, :], xn[:, ts, :], ALU.add).then_inc(s_x1, 1)
                pool.wait_ge(s_rgh, 1)
                nc.gpsimd.tensor_tensor(rg_l[:], rg_raw[:], rg_h[:], ALU.subtract).then_inc(s_rgl, 1)
                add_norm(0)
                ffn0.first_lows(pool)
                add_norm(1)

                def low_part(i, b, m):
                    cols = slice(m * WSTEP, (m + 1) * WSTEP)
                    pool.wait_ge(s_wh, i * WPARTS + (m + 1))
                    nc.gpsimd.tensor_tensor(w_l[b][:, cols], w_raw[b][:, cols], w_h[b][:, cols],
                                            ALU.subtract).then_inc(s_wl, 1)

                def cos_sin_low(i, m):
                    for w in range(2):
                        pool.wait_ge(s_crh, i * 12 + (2 * m + w + 1))
                        nc.gpsimd.tensor_tensor(qr_l[m % 2][:, w, :], qr[m % 2][:, w, :],
                                                qr_h[m % 2][:, w, :], ALU.subtract).then_inc(s_crl, 1)

                def slot(n, i, b, loads, do_s, do_q):
                    if do_q and n == F_AT:
                        pool.wait_ge(s_fh, i + 1)
                        nc.gpsimd.tensor_tensor(f_l[b][:], w_raw[b][:, FOFF:FW], f_h[b][:],
                                                ALU.subtract).then_inc(s_fl, 1)
                    if do_q and n in W_AT and not (isinstance(i, int) and i == NPAIR - 1):
                        low_part(i + 1, 1 - b, W_AT[n])
                    if q_here(n, i, do_q):
                        cos_sin_low(i, Q_AT[n])
                    if early(n, i, do_q):
                        cos_sin_low(i + 1, 0)

                def first_low_parts():
                    for m in range(WPARTS):
                        low_part(0, 0, m)
                pool.wait_ge(ffn0.hl, 1)
                ffn0.prog_pool(pool, {2 * N0 - 5: first_low_parts, 2 * N0 - 3: lambda: cos_sin_low(0, 0),
                                      2 * N0 - 2: lambda: cos_sin_low(0, 1)})
                run_pairs(slot, pool, {SLOTS - 1: lambda: ffn1.first_lows(pool)}, {})
                ffn1.prog_pool(pool, {})

            @block.tensor
            def _(pe):
                def fold(i):
                    b = i % 2
                    pe.wait_ge(s_pw[b], 32 * (i // 2 + 1))
                    for k in range(KD):
                        if i:
                            pe.wait_ge(s_fcp, 7 * (i - 1) + k + 1)
                        for h in range(2):
                            last = nc.tensor.matmul(bank[2 + k][:, h * CQ:(h + 1) * CQ], wq_of(b, h, k),
                                                    wkq_of(b, h), start=True, stop=True)
                        last.then_inc(s_f, 1)
                    if i:
                        pe.wait_ge(s_fcp, 7 * i)
                    for j in range(2 * JT):
                        bk, o = (bank[4], j * P) if j < 4 else (bank[7], (j - 4) * P)
                        src = (j % 2) * 2 * CQ + (j // 2) * P
                        nc.tensor.matmul(bk[:, o:o + P], pr[b][:, src:src + P],
                                         pr[b][:, 4 * CQ:4 * CQ + 2 * C], start=True, stop=True)
                    for h in range(2):
                        last = nc.tensor.matmul(bank[7][h * C:(h + 1) * C, D:2 * D], wkv_of(b, h),
                                                wo_of(b, h), start=True, stop=True, skip_group_check=True)
                    last.then_inc(s_f, 1)

                def add_transposed(b, bk):
                    pe.wait_ge(s_adj, b + 1)
                    for m in range(4):
                        c, r = m // 2, m % 2
                        nc.tensor.matmul(bank[bk][:, c * S + r * P:c * S + (r + 1) * P],
                                         adj[:, 2 * b + r, c * P:(c + 1) * P], ident[:],
                                         start=(m == 0), stop=False, is_transpose=True,
                                         skip_group_check=True)
                    nc.tensor.matmul(bank[bk][:], ident[:], adj[:, 2 * b:2 * b + 2, :],
                                     start=False, stop=True, skip_group_check=True).then_inc(s_adjT, 1)

                pe.wait_ge(s_const, 16)
                pe.wait_ge(s_ctx, 16)
                for t in range(NT):
                    last = nc.tensor.matmul(bank[t // 4][0:C, (t % 4) * P:(t % 4 + 1) * P], ctx_n[:, t, :],
                                            ident[:], start=True, stop=True, is_transpose=True)
                    if t % 4 == 3:
                        last.then_inc(s_ct, 1)
                pe.wait_ge(s_wqk, 16)
                nc.tensor.matmul(bank[2][0:C, 0:C], wqk[:, 0, :], wqk[:, 1, :],
                                 start=True, stop=True).then_inc(s_bm, 1)
                pe.wait_ge(s_bmc, 1)
                for c in range(NCH):
                    pe.wait_ge(s_ctc, c + 1)
                    nc.tensor.matmul(bank[3 + c][0:C, :], bmat[:], ctxT[:, c * 512:(c + 1) * 512],
                                     start=True, stop=True).then_inc(s_pt, 1)
                def similarity(g):
                    for t in (2 * g, 2 * g + 1):
                        pe.wait_ge(s_ptc, t // 4 + 1)
                        if t >= 4 and t % 2 == 0:
                            pe.wait_ge(s_simc, t // 2 - 1)
                        last = nc.tensor.matmul(bank[5 + g % 2][:, (t % 2) * S:(t % 2 + 1) * S],
                                                pT[:, t * P:(t + 1) * P], ctxT[:, g * S:(g + 1) * S],
                                                start=True, stop=True)
                    last.then_inc(s_sim, 1)
                similarity(0)
                similarity(1)
                pe.wait_ge(s_kv, 1)
                for t in range(NT):
                    last = nc.tensor.matmul(bank[t // 4][:, (t % 4) * P:(t % 4 + 1) * P], kv[:, t, :],
                                            ident[:], start=True, stop=True, is_transpose=True)
                last.then_inc(s_kvT, 1)
                pe.wait_ge(s_ptc, NCH)
                fold(0)
                similarity(2)
                similarity(3)
                fold(1)
                fold(2)
                pe.wait_ge(s_ksl, 1)
                add_transposed(0, 0)
                fold(3)
                fold(4)
                add_transposed(1, 1)
                fold(5)
                n_ffn0[0].pe_transpose(pe)
                route[0][0].pe_logits(pe)
                pe.wait_ge(s_upd, 2)
                ffn0.gateup(pe, ffn0_first)
                route[0][0].pe_turn_logits(pe)
                fold(6)
                rows_pe(route[0][0], pe)
                fold(7)
                pe.wait_ge(s_fcp, 7 * NPAIR)

                def transposed_second_half():
                    add_transposed(2, 6)
                    add_transposed(3, 7)

                def route_second_half():
                    n_ffn0[1].pe_transpose(pe)
                    route[0][1].pe_logits(pe)
                    route[0][1].pe_turn_logits(pe)

                def q_step(i, b, n, bk=None):
                    c, j = n // JT, n % JT
                    bk = n % 2 if bk is None else bk
                    if n == 0:
                        pe.wait_ge(s_wl, i * WPARTS + WPARTS)
                    if n >= 2 or not (isinstance(i, int) and i == 0):
                        pe.wait_ge(s_cs, i * 12 + 2 * (n - 1))
                    m = 0
                    for wp, xp in ((w_h, xT_h), (w_h, xT_l), (w_l, xT_h)):
                        for k in range(KD):
                            last = nc.tensor.matmul(bank[bk][:], m_of(wp[b], k, j),
                                                    xp[:, k, c * 512:(c + 1) * 512],
                                                    start=(m == 0), stop=(m == 5))
                            m += 1
                    last.then_inc(s_q, 1)

                def rope_step(i, b, n):
                    c, j = n // JT, n % JT
                    if j == 0 and not (isinstance(i, int) and i + c == 0):
                        pe.wait_ge(s_ql, i * 2 + c)
                    for w in range(2):
                        pe.wait_ge(s_crl, i * 12 + (2 * n + w + 1))
                        for m, (gp, qp) in enumerate(((w_h, qr_h), (w_h, qr_l), (w_l, qr_h))):
                            last = nc.tensor.matmul(bank[2][:], g_of(gp[b], 2 * j + w), qp[n % 2][:, w, :],
                                                    start=(j == w == m == 0),
                                                    stop=(j == JT - 1 and w == 1 and m == 2))
                    last.then_inc(s_rp, 1)

                def scores(j, jb, u):
                    if u % 4 == 0:
                        pe.wait_ge(s_ql, j * 2 + (u // 4 + 1))
                    keys = slice((u // 2) * S, (u // 2 + 1) * S)
                    for h in range(2):
                        o = bank[4 + u % 2][:, h * S:(h + 1) * S]
                        q = qs[jb][h][:, u * P:(u + 1) * P]
                        nc.tensor.matmul(o, q, ks_h[:, keys], start=True, stop=False)
                        last = nc.tensor.matmul(o, q, ks_l[:, keys], start=False, stop=True)
                    last.then_inc(s_sc, 1)

                def transpose_probs(j, u):
                    pe.wait_ge(s_pn, j * 8 + (u + 1))
                    pe.wait_ge(s_ev, j * 8 + (u + 1))
                    for h in range(2):
                        for k in range(2):
                            last = nc.tensor.matmul(bank[6][:, (2 * h + k) * P:(2 * h + k + 1) * P],
                                                    pn[u % 2][:, h, k * P:(k + 1) * P], ident[:],
                                                    start=True, stop=True, is_transpose=True)
                    last.then_inc(s_tr, 1)

                def values(j, b):
                    pe.wait_ge(s_ev, j * 8 + (2 * b + 3))
                    pe.wait_ge(s_cl, j * 4 + (b + 1))
                    for k in range(2):
                        for h in range(2):
                            last = nc.tensor.matmul(bank[7][h * C:(h + 1) * C, 0:S],
                                                    kv[:, 2 * b + k, 0:C], pT2[b % 2][:, h, k, :],
                                                    start=(k == 0), stop=(k == 1), skip_group_check=True)
                    last.then_inc(s_av, 1)

                def project(j, jb, b):
                    if b == 0:
                        pe.wait_ge(s_fl, j + 1)
                    pe.wait_ge(s_cl, j * 4 + (b + 2))
                    pe.wait_ge(s_xa, j * 4 + (b + 1))
                    for t in range(2):
                        for m, (cp, fp) in enumerate(((c_h, f_h), (c_h, f_l), (c_l, f_h))):
                            last = nc.tensor.matmul(bank[3][:, t * D:(t + 1) * D],
                                                    cp[b % 2][:, t * P:(t + 1) * P], fp[jb][:],
                                                    start=(m == 0), stop=(m == 2))
                    last.then_inc(s_y, 1)

                def slot(n, i, b, loads, do_s, do_q):
                    j, jb = i - 1, 1 - b
                    if do_s and LAG <= n < NU + LAG:
                        transpose_probs(j, n - LAG)
                    if do_s and n < NU:
                        scores(j, jb, n)
                    if do_q and n in R_AT:
                        rope_step(i, b, R_AT[n])
                    if q_here(n, i, do_q):
                        q_step(i, b, Q_AT[n])
                    if early(n, i, do_q):
                        q_step(i + 1, 1 - b, 0)
                    if do_s and n in VALUES_AT:
                        values(j, VALUES_AT[n])
                    if do_s and n in PROJECT_AT:
                        project(j, jb, PROJECT_AT[n])


                def first_q_step():
                    n_att[0].pe_whole(pe)
                    q_step(0, 0, 0, 6)
                pe.wait_ge(s_zr, 1)
                ffn0.prog_pe(pe, {N0 - 3: transposed_second_half, N0 - 1: route_second_half,
                                  N0: lambda: rows_pe(route[0][1], pe),
                                  N0 + 3: lambda: n_att[0].pe_transpose(pe), 2 * N0 - 4: first_q_step,
                                  2 * N0 - 3: lambda: q_step(0, 0, 1, 7)})


                def attention_to_ffn():
                    route[1][0].pe_logits(pe)
                    route[1][0].pe_turn_logits(pe)
                    ffn1.gateup(pe, ffn1_first)
                run_pairs(slot, pe, {Q3_AT - 1: lambda: n_att[1].pe_transpose(pe),
                                     Q3_AT: lambda: n_att[1].pe_whole(pe)},
                          {10: lambda: n_ffn1[0].pe_transpose(pe), 11: attention_to_ffn})
                pe.wait_ge(route[1][0].act, 1)
                pe.wait_ge(s_xa, NPAIR * B + 1)

                def logits_second_half():
                    route[1][1].pe_logits(pe)
                    route[1][1].pe_turn_logits(pe)
                ffn1.prog_pe(pe, {N1 - 2: lambda: n_ffn1[1].pe_transpose(pe),
                                  N1 - 1: logits_second_half})

            @block.scalar
            def _(act):
                for c in range(NCH):
                    act.wait_ge(s_ct, c + 1)
                    nc.scalar.activation(ctxT[:, c * 512:(c + 1) * 512], bank[c][0:C, :],
                                         ACT.Copy).then_inc(s_ctc, 1)
                act.wait_ge(s_bm, 1)
                nc.scalar.activation(bmat[:], bank[2][0:C, 0:C], ACT.Copy).then_inc(s_bmc, 1)
                for c in range(NCH):
                    act.wait_ge(s_pt, c + 1)
                    nc.scalar.activation(pT[:, c * 512:(c + 1) * 512], bank[3 + c][0:C, :],
                                         ACT.Copy).then_inc(s_ptc, 1)
                def similarity_out(g):
                    act.wait_ge(s_sim, g + 1)
                    for dst, s_done in ((left, s_left), (sim, s_simc)):
                        nc.scalar.activation(dst[:, 2 * g:2 * g + 2, :],
                                             bank[5 + g % 2][:].rearrange("p (t n) -> p t n", t=2),
                                             ACT.Copy).then_inc(s_done, 1)
                similarity_out(0)
                similarity_out(1)
                act.wait_ge(s_kvT, 1)
                for c in range(NCH):
                    last = nc.scalar.activation(ks_h[:, c * 512:(c + 1) * 512], bank[c][:], ACT.Copy)
                last.then_inc(s_ksh, 1)

                def fold_out(i):
                    f = w_raw[i % 2]
                    g4 = f[:, GOFF:FOFF].rearrange("p (j n) -> p j n", n=P)
                    b4 = bank[4][:].rearrange("p (j n) -> p j n", n=P)
                    b7 = bank[7][:].rearrange("p (j n) -> p j n", n=P)
                    if i >= 2:
                        act.wait_ge(s_stored[i % 2], 16 * (i // 2))
                    for k in range(KD):
                        act.wait_ge(s_f, 3 * i + k + 1)
                        nc.scalar.activation(f[:, k * 2 * CQ:(k + 1) * 2 * CQ], bank[2 + k][:, 0:2 * CQ],
                                             ACT.Copy).then_inc(s_fcp, 1)
                    act.wait_ge(s_f, 3 * i + 3)
                    for dst, src in ((g4[:, 0:2, 0:C], b4[:, 0:2, 0:C]), (g4[0:C, 2:4, 0:C], b4[0:C, 2:4, 0:C]),
                                     (g4[C:P, 2:4, C:P], b4[C:P, 2:4, C:P]), (g4[:, 4:6, C:P], b7[:, 0:2, C:P])):
                        nc.scalar.activation(dst, src, ACT.Copy).then_inc(s_fcp, 1)
                    last = nc.scalar.activation(f[:, FOFF:FW], bank[7][:, D:2 * D], ACT.Copy)
                    last.then_inc(s_fcp, 1)

                act.wait_ge(s_zero, 2)
                fold_out(0)
                similarity_out(2)
                similarity_out(3)
                act.wait_ge(s_simc, NT // 2)
                act.wait_ge(s_gates, 48)
                nc.scalar.activation(tg[:, 4:5], gates[:, 4:5], ACT.Sigmoid).then_inc(s_gact, 1)
                for g in range(NT // 2):
                    nc.scalar.activation(sig[:, 2 * g:2 * g + 2, :], sim[:, 2 * g:2 * g + 2, :],
                                         ACT.Sigmoid, scale=1.0 / 16.0).then_inc(s_sig, 1)
                nc.scalar.activation(tg[:, 0:4], gates[:, 0:4], ACT.Tanh).then_inc(s_gact, 1)
                act.wait_ge(s_rg, 16)
                nc.scalar.activation(rg_h[:], rg_raw[:], ACT.Copy).then_inc(s_rgh, 1)
                for hf in range(2):
                    n_l0att[hf].act_root(act)
                act.wait_ge(s_zz, 1)
                nc.scalar.activation(zero[:], hid[0][:], ACT.Copy).then_inc(s_zr, 1)
                for i in range(1, 4):
                    fold_out(i)
                ffn0.first_splits(act)
                for i in range(4, NPAIR - 2):
                    fold_out(i)
                n_ffn0[0].act_root(act)
                n_ffn0[0].act_high(act)
                route[0][0].act_logits(act)
                route0_act(route[0][0], act)
                fold_out(NPAIR - 2)
                ffn0.act_silu(act, ffn0_first)
                rows_act(route[0][0], act)
                ffn0.act_high(act, ffn0_first)
                fold_out(NPAIR - 1)

                def route_second_half():
                    n_ffn0[1].act_high(act)
                    route[0][1].act_logits(act)
                    route0_act(route[0][1], act)

                def cos_sin_high(i, n):
                    for w in range(2):
                        act.wait_ge(s_cs, i * 12 + (2 * n + w + 1))
                        nc.scalar.activation(qr_h[n % 2][:, w, :], qr[n % 2][:, w, :],
                                             ACT.Copy).then_inc(s_crh, 1)

                def q_high(i, b, c):
                    act.wait_ge(s_rp, i * 6 + (3 * c + 3))
                    for h in range(2):
                        last = nc.scalar.activation(qs[b][h][0:C, c * 512:(c + 1) * 512],
                                                    bank[2][h * C:(h + 1) * C, :], ACT.Copy)
                    last.then_inc(s_qh, 1)

                def exps(j, u):
                    act.wait_ge(s_nm, j * 8 + (u + 1))
                    for h in range(2):
                        last = nc.scalar.activation(ex[u % 2][:, h, :], bank[4 + u % 2][:, h * S:(h + 1) * S],
                                                    ACT.Exp, bias=negm[:, u % 2, h:h + 1],
                                                    accum_out=den[:, u % 2, h:h + 1])
                    last.then_inc(s_ex, 1)

                def probs_out(j, u):
                    act.wait_ge(s_tr, j * 8 + (u + 1))
                    r = u % 2
                    nc.scalar.activation(pT2[(u // 2) % 2][:, :, :, r * P:(r + 1) * P],
                                         bank[6][:].rearrange("p (h k n) -> p h k n", h=2, k=2),
                                         ACT.Copy).then_inc(s_ev, 1)

                def values_high(j, b):
                    act.wait_ge(s_av, j * 4 + (b + 1))
                    nc.scalar.activation(c_h[b % 2][:], bank[7][:, 0:S], ACT.Copy).then_inc(s_ch, 1)

                def high_part(i, b, loads, m):
                    cols = slice(m * WSTEP, (m + 1) * WSTEP)
                    if m == 0 and isinstance(i, int) and i < 2:
                        act.wait_ge(s_fcp, 7 * NPAIR)
                    elif m == 0:
                        act.wait_ge(s_w[b], (loads - 1) * 16)
                    nc.scalar.activation(w_h[b][:, cols], w_raw[b][:, cols], ACT.Copy).then_inc(s_wh, 1)

                def slot(n, i, b, loads, do_s, do_q):
                    j = i - 1
                    if do_q and n in QH_AT:
                        q_high(i, b, QH_AT[n])
                    if do_s and LAG <= n < NU + LAG:
                        probs_out(j, n - LAG)
                    if do_s and n < NU:
                        exps(j, n)
                    if do_q and n == F_AT:
                        nc.scalar.activation(f_h[b][:], w_raw[b][:, FOFF:FW], ACT.Copy).then_inc(s_fh, 1)
                    if do_q and n in W_AT and not (isinstance(i, int) and i == NPAIR - 1):
                        high_part(i + 1, 1 - b, loads + b, W_AT[n])
                    if q_here(n, i, do_q):
                        cos_sin_high(i, Q_AT[n])
                    if early(n, i, do_q):
                        cos_sin_high(i + 1, 0)
                    if do_s and n in VALUES_AT:
                        values_high(j, VALUES_AT[n])


                def first_high_parts():
                    for m in range(WPARTS):
                        high_part(0, 0, 1, m)
                ffn0.prog_act(act, {N0 - 2: lambda: n_ffn0[1].act_root(act), N0 - 1: route_second_half,
                                    N0 + 2: lambda: n_att[0].act_root(act), N0 + 3: lambda: n_att[0].act_high(act),
                                    2 * N0 - 5: first_high_parts, 2 * N0 - 3: lambda: cos_sin_high(0, 0),
                                    2 * N0 - 2: lambda: cos_sin_high(0, 1)},
                              {N0 - 1: lambda: rows_act(route[0][1], act)})

                def split_first_tile():
                    act.wait_ge(ffn0.down, 2 * N0)
                    ffn1.first_splits(act)

                def route_first_half():
                    route[1][0].act_logits(act)
                    route1_act(route[1][0], act)
                act.sem_inc(s_ev, 1)
                n_att[1].act_root(act)
                run_pairs(slot, act, {Q3_AT - 1: lambda: n_att[1].act_high(act), 9: split_first_tile},
                          {9: lambda: n_ffn1[0].act_root(act), 10: lambda: n_ffn1[0].act_high(act),
                           11: route_first_half})
                ffn1.act_silu(act, ffn1_first)
                ffn1.act_high(act, ffn1_first)

                def route_last_half():
                    route[1][1].act_logits(act)
                    route1_act(route[1][1], act)
                ffn1.prog_act(act, {N1 - 3: lambda: n_ffn1[1].act_root(act),
                                    N1 - 2: lambda: n_ffn1[1].act_high(act),
                                    N1 - 1: route_last_half}, {})

            @block.vector
            def _(dve):
                seq = Seq(dve, "vector_step")
                dve.wait_ge(s_ctx, 16)
                dve.wait_ge(s_trigk, 16)
                c4 = ctx_n[:].rearrange("p (b r) d -> p b r d", b=B)
                k4 = kvc[:].rearrange("p (b r) d -> p b r d", b=B)
                s4 = kvs[:].rearrange("p (b r) d -> p b r d", b=B)
                hc = C // 2

                def tab(which, lo, hi):
                    return trigk[:, which, :, lo:hi].unsqueeze(1).broadcast_to([P, B, 2, hi - lo])
                seq.did(nc.vector.tensor_tensor(k4, c4, tab(0, 0, C), ALU.mult))
                seq.did(nc.vector.tensor_tensor(s4[:, :, :, 0:hc], c4[:, :, :, hc:C], tab(1, 0, hc), ALU.mult))
                seq.link(nc.vector.tensor_tensor(s4[:, :, :, hc:C], c4[:, :, :, 0:hc], tab(1, hc, C), ALU.mult))
                for h in range(2):
                    last = nc.vector.tensor_tensor(kv[:, :, h * C:(h + 1) * C], kvc[:], kvs[:], ALU.add)
                last.then_inc(s_kv, 1)
                dve.wait_ge(s_x, 16)
                for hf in range(2):
                    n_l0att[hf].stats(seq)

                def topk(g):
                    pair = (2 * g, 2 * g + 1)
                    dve.wait_ge(s_left, g + 1)
                    for r in range(rounds):
                        for t in pair:
                            if r:
                                dve.wait_ge(seq.sem, seq.n - 1)
                            seq.did(nc.vector.max(best[:, t, :], left[:, t, :]))
                        if r < rounds - 1:
                            for t in pair:
                                dve.wait_ge(seq.sem, seq.n - 1)
                                seq.did(nc.vector.match_replace(left[:, t, :], best[:, t, :], left[:, t, :], NEG))
                    seq.wait()

                def threshold(g):
                    dve.wait_ge(s_simc, g + 1)
                    dve.wait_ge(s_sig, g + 1)
                    for t in (2 * g, 2 * g + 1):
                        least = best[:, t, kth:kth + 1] if t < HN else kept[:, t - HN:t - HN + 1]
                        last = nc.vector.scalar_tensor_tensor(
                            out=adj[:, t, :], in0=sim[:, t, :], scalar=least,
                            in1=sig[:, t, :], op0=ALU.is_ge, op1=ALU.mult)
                    last.then_inc(s_adj, 1)

                def update(g, bk):
                    dve.wait_ge(s_adjT, g + 1)
                    dve.wait_ge(s_x1, g + 1)
                    nc.vector.scalar_tensor_tensor(
                        out=x[:, 2 * g:2 * g + 2, :], in0=bank[bk][:].rearrange("p (t n) -> p t n", t=2),
                        scalar=cc[:, 2:3], in1=x[:, 2 * g:2 * g + 2, :],
                        op0=ALU.mult, op1=ALU.add).then_inc(s_upd, 1)

                topk(0)
                threshold(0)
                dve.wait_ge(s_ksh, 1)
                for c in range(NCH):
                    last = nc.vector.tensor_tensor(ks_l[:, c * 512:(c + 1) * 512], bank[c][:],
                                                   ks_h[:, c * 512:(c + 1) * 512], ALU.subtract)
                last.then_inc(s_ksl, 1)
                dve.wait_ge(s_gact, 2)
                seq.link(nc.vector.tensor_tensor(cc[:, 0:1], tg[:, 0:1], tg[:, 4:5], ALU.mult))
                seq.did(nc.vector.tensor_tensor(cc[:, 1:2], tg[:, 0:1], cc[:, 0:1], ALU.subtract))
                seq.link(nc.vector.tensor_scalar(cc[:, 2:3], cc[:, 0:1], 0.5, None, ALU.mult))
                n_l0att[0].scale(dve, seq)
                topk(1)
                threshold(1)
                update(0, 0)
                update(1, 1)
                dve.wait_ge(s_upd, 2)
                n_ffn0[0].stats(seq)
                n_ffn0[0].scale(dve, seq)
                n_ffn0[0].low(dve)
                n_l0att[1].scale(dve, seq)
                route0(route[0][0], dve, seq)
                dve.wait_ge(route[0][0].rowc, 1)
                ffn0.hidden(dve, ffn0_first)
                ffn0.low(dve, nc.vector, ffn0_first)
                dve.wait_ge(s_left, NT // 2)

                def topk_round(st, part):
                    if st.c >= rounds:
                        return
                    if part == 0 and (st.loop or st.k):
                        dve.wait_ge(s_rep, st.k * HN)
                    for t in range(HN, NT):
                        if part == 1:
                            nc.vector.max(best[:, t, :], left[:, t, :]).then_inc(s_top, 1)
                    if part == 1:
                        dve.wait_ge(s_top, st.k * HN + HN)
                        nc.vector.tensor_copy(kept[:], best[:, HN:NT, kth]).then_inc(s_kept, 1)
                        for t in range(HN, NT):
                            nc.vector.match_replace(left[:, t, :], best[:, t, :], left[:, t, :],
                                                    NEG).then_inc(s_rep, 1)

                def threshold_second_half():
                    dve.wait_ge(s_rep, rounds * HN)
                    dve.wait_ge(s_kept, rounds)
                    threshold(2)
                    threshold(3)

                def update_second_half():
                    update(2, 6)
                    update(3, 7)
                    dve.wait_ge(s_upd, B)
                    n_ffn0[1].stats(seq)

                def route_second_half():
                    n_ffn0[1].low(dve)
                    route0(route[0][1], dve, seq)
                    dve.wait_ge(route[0][1].rowc, 2)

                def norm_first_half():
                    dve.wait_ge(ffn0.acc, 1)
                    n_att[0].stats(seq)

                def first_cos_sin():
                    dve.wait_ge(s_trig, 32)
                    cos_sin(0, 0, 6)
                def cos_sin(i, n, bk=None):
                    dve.wait_ge(s_q, i * 6 + (n + 1))
                    q2 = bank[n % 2 if bk is None else bk][:].rearrange("p (b s) -> p b s", b=2)
                    for w, tab in ((0, cosq), (1, sinq)):
                        nc.vector.tensor_tensor(qr[n % 2][:, w, :].rearrange("p (b s) -> p b s", b=2), q2,
                                                tab[:, n % JT:n % JT + 1, :].broadcast_to([P, 2, S]),
                                                ALU.mult).then_inc(s_cs, 1)

                def q_low(i, b, c):
                    dve.wait_ge(s_qh, i * 2 + (c + 1))
                    for h in range(2):
                        cols = slice(c * 512, (c + 1) * 512)
                        last = nc.vector.tensor_tensor(qs[b][h][C:P, cols], bank[2][h * C:(h + 1) * C, :],
                                                       qs[b][h][0:C, cols], ALU.subtract)
                    last.then_inc(s_ql, 1)

                def maxima(j, u):
                    dve.wait_ge(s_sc, j * 8 + (u + 1))
                    nc.vector.tensor_reduce(negm[:, u % 2, :], bank[4 + u % 2][:].rearrange(
                        "p (h n) -> p h n", h=2), AX_X, ALU.max, negate=True).then_inc(s_nm, 1)

                def normalise(j, u):
                    dve.wait_ge(s_ex, j * 8 + (u + 1))
                    nc.vector.reciprocal(rden[:, u % 2, :], den[:, u % 2, :]).then_inc(s_rd, 1)
                    dve.wait_ge(s_rd, j * 8 + (u + 1))
                    for h in range(2):
                        last = nc.vector.tensor_scalar(pn[u % 2][:, h, :], ex[u % 2][:, h, :],
                                                       rden[:, u % 2, h:h + 1], None, ALU.mult)
                    last.then_inc(s_pn, 1)

                def values_low(j, b):
                    dve.wait_ge(s_ch, j * 4 + (b + 1))
                    nc.vector.tensor_tensor(c_l[b % 2][:], bank[7][:, 0:S], c_h[b % 2][:],
                                            ALU.subtract).then_inc(s_cl, 1)

                def add(j, b):
                    dve.wait_ge(s_y, j * 4 + (b + 1))
                    nc.vector.scalar_tensor_tensor(
                        out=x[:, 2 * b:2 * b + 2, :], in0=bank[3][:].rearrange("p (t d) -> p t d", t=2),
                        scalar=tg[:, 1:2], in1=x[:, 2 * b:2 * b + 2, :],
                        op0=ALU.mult, op1=ALU.add).then_inc(s_xa, 1)

                def slot(n, i, b, loads, do_s, do_q):
                    j = i - 1
                    if do_s and n < NU:
                        maxima(j, n)
                    if do_s and 1 <= n <= NU:
                        normalise(j, n - 1)
                    if do_q and n in QH_AT:
                        q_low(i, b, QH_AT[n])
                    if q_here(n, i, do_q):
                        cos_sin(i, Q_AT[n])
                    if early(n, i, do_q):
                        cos_sin(i + 1, 0)
                    if do_s and n in VALUES_AT:
                        values_low(j, VALUES_AT[n])
                    if do_s and n in PROJECT_AT:
                        add(j, PROJECT_AT[n])

                ffn0.prog_dve(dve, {N0 - 4: threshold_second_half, N0 - 3: update_second_half,
                                    N0 - 2: lambda: n_ffn0[1].scale(dve, seq), N0 - 1: route_second_half,
                                    N0 + 1: norm_first_half, N0 + 2: lambda: n_att[0].scale(dve, seq),
                                    N0 + 3: lambda: n_att[0].low(dve), 2 * N0 - 4: first_cos_sin,
                                    2 * N0 - 3: lambda: cos_sin(0, 1, 7)}, topk_round)

                dve.sem_inc(s_cl, 1)
                dve.sem_inc(s_xa, 1)
                dve.wait_ge(ffn0.acc, 2)
                n_att[1].stats(seq)
                n_att[1].scale(dve, seq)

                def norm_for_ffn():
                    dve.wait_ge(s_xa, (NPAIR - 1) * B + 3)
                    n_ffn1[0].stats(seq)
                run_pairs(slot, dve, {Q3_AT - 1: lambda: n_att[1].low(dve)},
                          {8: norm_for_ffn, 9: lambda: n_ffn1[0].scale(dve, seq), 10: lambda: n_ffn1[0].low(dve)})
                ffn1.hidden(dve, ffn1_first)
                ffn1.low(dve, nc.vector, ffn1_first)
                route1(route[1][0], dve, seq)

                def norm_second_half():
                    dve.wait_ge(s_xa, NPAIR * B + 1)
                    n_ffn1[1].stats(seq)
                ffn1.prog_dve(dve, {1: norm_second_half, N1 - 3: lambda: n_ffn1[1].scale(dve, seq),
                                    N1 - 2: lambda: n_ffn1[1].low(dve),
                                    N1: lambda: route1(route[1][1], dve, seq)}, lambda st, part: None)


def rope_tables(length, dim):
    inv = (1.0 / 10000.0 ** (np.arange(0, dim, 2, dtype=np.float32) / np.float32(dim))).astype(np.float32)
    f = np.arange(length, dtype=np.float32)[:, None] * inv[None, :]
    return np.repeat(np.sin(f), 2, axis=-1).astype(np.float32), np.repeat(np.cos(f), 2, axis=-1).astype(np.float32)


def constants():
    sq, cq = rope_tables(S, CQ)
    half = CQ // 2
    turned = (np.arange(CQ) + half) % CQ
    sign = np.where(np.arange(CQ) < half, 1.0, -1.0).astype(np.float32)
    sq_m = (sq[:, turned] * sign[None, :]).T
    pack = lambda t: np.concatenate([t, t]).reshape(JT, P, S).transpose(1, 0, 2)
    sk, ck = rope_tables(S, C)
    sk = sk * np.where(np.arange(C) < C // 2, -1.0, 1.0).astype(np.float32)[None, :]
    trigk = np.stack([ck, sk]).reshape(2, 2, P, C).transpose(2, 0, 1, 3)
    sel0 = np.zeros((E0, P), np.float32)
    for e in range(E0):
        sel0[e, e * (P // E0):(e + 1) * (P // E0)] = 1.0
    return {
        "ident": np.eye(P, dtype=np.float32), "iota": np.arange(E1, dtype=np.float32), "sel0": sel0,
        "cosq": pack(cq.T), "sinq": pack(sq_m), "trigk": trigk,
    }


def layouts(v):
    g = {}
    tiles = lambda t: t.reshape(NT, P, -1).transpose(1, 0, 2)
    g["x"] = tiles(v["x"])
    g["ctx"] = tiles(v["ctx_512"])
    g["wqk"] = np.stack([v["L0_xattn_Wq"], v["L0_xattn_Wk"]], axis=1)
    g["gates"] = np.concatenate([v["g_xattn"], v["g_ffn"], v["L0_xattn_gamma_raw"].reshape(1)])
    r0 = np.zeros((D, E1), np.float32)
    r0[:, 0:E0] = v["L0_ffn_gate_weight"].T
    g["router"] = np.stack([r0, v["L1_ffn_gate_w"]]).reshape(2, KD, P, E1).transpose(2, 0, 1, 3)
    g["bias1"] = v["L1_ffn_expert_bias"]

    def ffn_tile(gate, up, down):
        return np.concatenate([gate[0:P], up[0:P], gate[P:D], up[P:D], down], axis=1)

    gu = v["L0_ffn_gate_up_weights"]
    gate = gu[:, 0:F0].reshape(P, R0, D)
    up = gu[:, F0:2 * F0].reshape(P, R0, D)
    down = v["L0_ffn_down_weights"].transpose(0, 2, 1).reshape(P, R0, D)
    w = [ffn_tile(gate[:, t].T, up[:, t].T, down[:, t]) for t in range(R0)]
    rows = (N0 - R0) * P
    sgu = np.zeros((2, rows, D), np.float32)
    sgu[:, 0:FS0] = v["L0_ffn_shared_gate_up"].reshape(2, FS0, D)
    sd = np.zeros((rows, D), np.float32)
    sd[0:FS0] = v["L0_ffn_shared_down"].T
    for t in range(N0 - R0):
        s = slice(t * P, (t + 1) * P)
        w.append(ffn_tile(sgu[0, s].T, sgu[1, s].T, sd[s]))
    g["w_ffn0"] = np.stack(w)
    gu1 = v["L1_ffn_experts_gate_up"]
    w = [ffn_tile(gu1[e, :, 0:F1], gu1[e, :, F1:], v["L1_ffn_experts_down"][e]) for e in range(E1)]
    w.append(ffn_tile(v["L1_ffn_shared_gate_w"], v["L1_ffn_shared_up_w"], v["L1_ffn_shared_down_w"]))
    g["w_ffn1"] = np.stack(w)

    wq = v["L1_xattn_Wq"].reshape(H, KH, D)
    wo = v["L1_xattn_Wo"].T.reshape(H, KH, D)
    turned = (np.arange(CQ) + CQ // 2) % CQ
    pw, pr = [], []
    for i in range(NPAIR):
        h0, h1 = 2 * i, 2 * i + 1
        pw.append(np.concatenate([wq[h0], wq[h1], v["L1_xattn_w_kc_q"][h0], v["L1_xattn_w_kc_q"][h1],
                                  v["L1_xattn_w_kc_kv"][h0], v["L1_xattn_w_kc_kv"][h1], wo[h0], wo[h1]], axis=1))
        qr = [v["L1_xattn_W_qr"][h].T for h in (h0, h1)]
        kr = [v["L1_xattn_W_kr"][h].T for h in (h0, h1)]
        pr.append(np.concatenate([qr[0], qr[1], qr[0][:, turned], qr[1][:, turned], kr[0], kr[1]], axis=1))
    g["pair_w"] = np.stack(pw)
    g["pair_r"] = np.stack(pr)
    return g


def kernel(**inputs):
    import concourse.bacc as bacc
    from concourse.bass_utils import run_bass_kernel_spmd

    arrays = {**layouts({k: np.asarray(v) for k, v in inputs.items()}), **constants()}
    arrays = {k: np.ascontiguousarray(v) for k, v in arrays.items()}
    nc = bacc.Bacc("TRN2", target_bir_lowering=False, num_devices=1)
    aps = {k: nc.dram_tensor(f"in_{k}", v.shape, F32, kind="ExternalInput").ap() for k, v in arrays.items()}
    out = nc.dram_tensor("out", (P, NT, D), F32, kind="ExternalOutput").ap()
    build(nc, aps, out)
    r = run_bass_kernel_spmd(nc, [{f"in_{k}": v for k, v in arrays.items()}], core_ids=[0])
    return r.results[0]["out"].transpose(1, 0, 2).reshape(B, S, D)
```
